# Optimizing a Trainium2 kernel written in Bass

```python
import numpy as np
import jax
import jax.numpy as jnp

def _softmax(x, axis=-1):
    return jax.nn.softmax(x, axis=axis)
def _gelu(x):
    return jax.nn.gelu(x, approximate=True)
def _silu(x):
    return jax.nn.silu(x)
def _sigmoid(x):
    return jax.nn.sigmoid(x)
def _layernorm(x, axis=-1, eps=1e-5):
    m = jnp.mean(x, axis=axis, keepdims=True)
    v = jnp.var(x, axis=axis, keepdims=True)
    return (x - m) / jnp.sqrt(v + eps)
def _scatter_add(tgt, idx, src, axis=0):
    return tgt.at[idx].add(src)
def _segment_sum(src, seg, n):
    return jax.ops.segment_sum(src, seg, n)

kernel_name = 'mk_conv_preact_d1_conv_nhwc768_9e1717'

def setup_inputs(seed: int = 0):
    np.random.seed(seed)
    _w = jnp.asarray
    def _rec_inputs():
        import jax
        import jax.numpy as jnp
        _gk = jax.random.key(seed)
        x = -0.0001538 + 1 * jax.random.normal(jax.random.fold_in(_gk, 1), (8, 32, 32, 768), jnp.float32)
        return x
    x = _rec_inputs()
    def _L0_conv_setup():
        import jax, jax.numpy as jnp
        import numpy as np
        B, Hs, Ws, DIM = (8, 32, 32, 768)
        NH, HD = (12, 64)

        def get_rel_pos(size, rel_pos):
            coords = jnp.arange(size)[:, None] - jnp.arange(size)[None, :] + (size - 1)
            return rel_pos[coords]
        key = jax.random.key(seed)
        ks = jax.random.split(key, 7)
        inv = 1.0 / np.sqrt(DIM)
        return {'x': jax.random.normal(ks[0], (B, Hs, Ws, DIM), jnp.float32), 'qkv_w': jax.random.normal(ks[1], (3 * DIM, DIM), jnp.float32) * inv, 'qkv_b': jax.random.normal(ks[2], (3 * DIM,), jnp.float32) * 0.02, 'proj_w': jax.random.normal(ks[3], (DIM, DIM), jnp.float32) * inv, 'proj_b': jax.random.normal(ks[4], (DIM,), jnp.float32) * 0.02, 'rel_pos_h': jax.random.normal(ks[5], (2 * Hs - 1, HD), jnp.float32) * 0.02, 'rel_pos_w': jax.random.normal(ks[6], (2 * Ws - 1, HD), jnp.float32) * 0.02}
    _L0_conv_all = _L0_conv_setup()
    _L0_conv_in = {k: v for k, v in _L0_conv_all.items() if k in ('qkv_w', 'qkv_b', 'proj_w', 'proj_b', 'rel_pos_h', 'rel_pos_w', )}
    del _L0_conv_all

    return {
        "x": x,
        "L0_conv_qkv_w": _L0_conv_in["qkv_w"],
        "L0_conv_qkv_b": _L0_conv_in["qkv_b"],
        "L0_conv_proj_w": _L0_conv_in["proj_w"],
        "L0_conv_proj_b": _L0_conv_in["proj_b"],
        "L0_conv_rel_pos_h": _L0_conv_in["rel_pos_h"],
        "L0_conv_rel_pos_w": _L0_conv_in["rel_pos_w"],
    }

def reference(x, L0_conv_qkv_w, L0_conv_qkv_b, L0_conv_proj_w, L0_conv_proj_b, L0_conv_rel_pos_h, L0_conv_rel_pos_w):
    import jax
    import jax.numpy as jnp
    def _L0_conv_ref(x, qkv_w, qkv_b, proj_w, proj_b, rel_pos_h, rel_pos_w):
        import jax, jax.numpy as jnp
        import numpy as np
        B, Hs, Ws, DIM = (8, 32, 32, 768)
        NH, HD = (12, 64)

        def get_rel_pos(size, rel_pos):
            coords = jnp.arange(size)[:, None] - jnp.arange(size)[None, :] + (size - 1)
            return rel_pos[coords]
        Bb, H, W, C = x.shape
        L = H * W
        scale = HD ** (-0.5)
        qkv = x @ qkv_w.T + qkv_b
        qkv = qkv.reshape(Bb, L, 3, NH, HD).transpose(2, 0, 3, 1, 4)
        q, k, v = (qkv[0], qkv[1], qkv[2])
        rel_h = get_rel_pos(H, rel_pos_h)
        rel_w = get_rel_pos(W, rel_pos_w)
        q5 = q.reshape(Bb, NH, H, W, HD)
        rel_h_attn = jnp.einsum('bnhwc,hkc->bnhwk', q5, rel_h)
        rel_w_attn = jnp.einsum('bnhwc,wkc->bnhwk', q5, rel_w)
        bias = rel_h_attn[..., :, None] + rel_w_attn[..., None, :]
        bias = bias.reshape(Bb, NH, L, L)
        scores = jnp.einsum('bnqd,bnkd->bnqk', q, k) * scale + bias
        attn = jax.nn.softmax(scores, axis=-1)
        out = jnp.einsum('bnqk,bnkd->bnqd', attn, v)
        out = out.reshape(Bb, NH, H, W, HD).transpose(0, 2, 3, 1, 4).reshape(Bb, H, W, C)
        return out @ proj_w.T + proj_b

    def _gn(v, G=32, eps=1e-5):
        B_, H_, W_, C_ = v.shape
        g = v.reshape(B_, H_, W_, G, C_ // G)
        m = jnp.mean(g, axis=(1, 2, 4), keepdims=True)
        s = jnp.var(g, axis=(1, 2, 4), keepdims=True)
        return ((g - m) / jnp.sqrt(s + eps)).reshape(v.shape)

    def _ln_c(v, eps=1e-6):
        m = jnp.mean(v, axis=-1, keepdims=True)
        s = jnp.var(v, axis=-1, keepdims=True)
        return (v - m) / jnp.sqrt(s + eps)

    def _ln_t(v, eps=1e-5):
        m = jnp.mean(v, axis=-1, keepdims=True)
        s = jnp.var(v, axis=-1, keepdims=True)
        return (v - m) / jnp.sqrt(s + eps)

    def _to_tokens(v):
        B_, H_, W_, C_ = v.shape
        return v.reshape(B_, H_ * W_, C_)
    def _from_tokens(t, like):
        return t.reshape(like.shape)

    x = x + _L0_conv_ref(_gn(x), L0_conv_qkv_w, L0_conv_qkv_b, L0_conv_proj_w, L0_conv_proj_b, L0_conv_rel_pos_h, L0_conv_rel_pos_w)
    return x


_drawn_inputs = setup_inputs


def setup_inputs(seed=0):
    import zlib

    import numpy as np

    out = dict(_drawn_inputs(seed))
    spreads = {}
    factors = {'L0_conv_qkv_b': 2.739,
     'L0_conv_proj_b': 2.841,
     'L0_conv_rel_pos_h': 3.294,
     'L0_conv_rel_pos_w': 2.838}
    for name, (base, spread) in spreads.items():
        noise = np.random.default_rng([zlib.crc32(name.encode()), seed]).standard_normal(out[name].shape)
        drawn = base * np.exp(spread * noise) if base else spread * noise
        out[name] = jnp.asarray(drawn.astype(out[name].dtype))
    for name, factor in factors.items():
        out[name] = (out[name] * factor).astype(out[name].dtype)
    return out
```

```python
from contextlib import ExitStack

import numpy as np
import concourse.bass as bass
from concourse import mybir

F32 = mybir.dt.float32
F32R = mybir.dt.float32r
ACT = mybir.ActivationFunctionType
ALU = mybir.AluOpType
AX_X = mybir.AxisListType.X

P = 128
B, HS, WS, C = 8, 32, 32, 768
T = HS * WS
HALF = T // 2
NH, D = 12, 64
NPAIR = NH // 2
NIT = B * NPAIR
CB = C // P
KB = T // P
NREL = 2 * HS - 1
GROUP = C // 32
PER_GROUP = GROUP // CB
EPS = 1e-5
SCALE = float(D) ** -0.5


def positive(value):
    return not isinstance(value, int) or value > 0


def words(ap):
    return ap.bitcast(F32)


def project_qkv(nc, x_t, w_t, bias_cols, group_mean, qk_hi, qk_lo, v_rows):
    QK = 2 * CB
    VN = C // 2
    VG = 2 * (HALF // P)
    NG = QK + VG
    BANKS, SLOTS = 5, 4
    with ExitStack() as ctx:
        sb = lambda name, shape, dt: ctx.enter_context(nc.sbuf_tensor(name, shape, dt))
        sem = lambda name: ctx.enter_context(nc.semaphore(name))
        w_hi = sb("w_hi", [P, CB, 3 * C], F32R)
        w_lo = sb("w_lo", [P, CB, 3 * C], F32R)
        x_hi = sb("x_hi", [P, 2, CB, HALF], F32R)
        x_lo = sb("x_lo", [P, 2, CB, HALF], F32R)
        x_raw = sb("x_raw", [P, CB, T], F32)
        out_hi = sb("out_hi", [P, SLOTS, HALF], F32R)
        out_lo = sb("out_lo", [P, SLOTS, HALF], F32R)
        out_v = sb("out_v", [P, SLOTS, VN], F32)
        bias = sb("bias", [P, QK], F32)
        mean4 = sb("mean4", [P, P], F32)
        stats = sb("stats", [P, 2 * CB, 6], F32)
        moments = sb("moments", [P, 2], F32)
        gmean = sb("gmean", [P, 2], F32)
        shift = sb("shift", [P, 2], F32)
        spread = sb("spread", [P, 2], F32)
        gvar = sb("gvar", [P, 2], F32)
        std = sb("std", [P, 2], F32)
        rstd = sb("rstd", [P, 2], F32)
        ps = ctx.enter_context(nc.psum_tensor("ps_qkv", [P, BANKS, HALF], F32))
        ps_stat = ctx.enter_context(nc.psum_tensor("ps_stat", [P, HALF], F32))
        w_stage = x_raw[:, :, :].rearrange("p k t -> p (k t)")

        consts_in = sem("p1_consts_in")
        w_in = [sem(f"w_in{i}") for i in range(2)]
        w_hi_done, w_lo_done = sem("w_hi_done"), sem("w_lo_done")
        x_in = sem("x_in")
        dve_step = sem("dve_step")
        part_mean, gmean_ps, part_var, gvar_ps = sem("part_mean"), sem("gmean_ps"), sem("part_var"), sem("gvar_ps")
        var_ready, std_ready = sem("var_ready"), sem("std_ready")
        x_normed, x_hi_done, x_lo_done = sem("x_normed"), sem("x_hi_done"), sem("x_lo_done")
        group_done = sem("group_done")
        hi_out, lo_out = sem("hi_out"), sem("lo_out")
        v_out = sem("v_out")
        qk_stored = [sem(f"qk_stored{i}") for i in range(SLOTS)]
        v_stored = [sem(f"v_stored{i}") for i in range(SLOTS)]
        block = ctx.enter_context(nc.Block())
        k_cols = slice(C, 2 * C)
        plain_cols = (slice(0, C), slice(2 * C, 3 * C))

        @block.sync
        def _(sp):
            sp.dma_start(bias[:, :], bias_cols).then_inc(consts_in, 16)
            sp.dma_start(mean4[:, :], group_mean).then_inc(consts_in, 16)
            w_rows = w_t.rearrange("(p k) n -> p k n", k=CB)
            for k in range(CB):
                if k >= 2:
                    sp.wait_ge(w_lo_done, 3 * (k - 1))
                s = k % 2
                sp.dma_start(w_stage[:, s * 3 * C:(s + 1) * 3 * C], w_rows[:, k, :]).then_inc(w_in[s], 16)
            sp.wait_ge(w_lo_done, 3 * CB)
            sp.dma_start(x_raw[:, :, :], x_t[0].rearrange("(p k) t -> p k t", k=CB)).then_inc(x_in, 16)

            def image(i, last):
                for h in range(2):
                    n = 2 * i + h
                    for g in range(QK):
                        sp.wait_ge(lo_out, n * QK + g + 1)
                        rows = slice((g % CB) * P, (g % CB + 1) * P)
                        cols = slice(h * HALF, (h + 1) * HALF)
                        s = g % SLOTS
                        sp.dma_start(qk_hi[g // CB][i, rows, cols], words(out_hi[:, s, :])).then_inc(qk_stored[s], 16)
                        sp.dma_start(qk_lo[g // CB][i, rows, cols], words(out_lo[:, s, :])).then_inc(qk_stored[s], 16)
                        if h == 0 and g == 1 and not last:
                            sp.wait_ge(x_lo_done, 2 * i + 2)
                            sp.dma_start(x_raw[:, :, :], x_t[i + 1].rearrange("(p k) t -> p k t", k=CB)).then_inc(x_in, 16)
                    for g in range(VG):
                        sp.wait_ge(v_out, VG + n * VG + g + 1)
                        kb, c = h * (HALF // P) + g // 2, g % 2
                        dst = v_rows[i, c * (NPAIR // 2):(c + 1) * (NPAIR // 2), :, kb, :].rearrange("j p d -> p j d")
                        sp.dma_start(dst, out_v[:, g % SLOTS, :].rearrange("p (j d) -> p j d", d=P)).then_inc(v_stored[g % SLOTS], 16)
            image(0, False)
            with sp.Fori(1, B - 1) as i:
                image(i, False)
            image(B - 1, True)
            for s in range(SLOTS):
                sp.wait_ge(qk_stored[s], 32 * 2 * B * QK // SLOTS)
                sp.wait_ge(v_stored[s], 16 * 2 * B * VG // SLOTS)

        @block.scalar
        def _(act):
            act.sem_inc(v_out, VG)
            for k in range(CB):
                act.wait_ge(w_in[k % 2], 16 * (k // 2 + 1))
                st = w_stage[:, (k % 2) * 3 * C:(k % 2 + 1) * 3 * C]
                for cols in plain_cols:
                    nc.scalar.activation(w_hi[:, k, cols], st[:, cols], ACT.Identity).then_inc(w_hi_done, 1)
                nc.scalar.activation(w_hi[:, k, k_cols], st[:, k_cols], ACT.Identity, scale=SCALE).then_inc(w_hi_done, 1)

            def deviation(i):
                act.wait_ge(var_ready, i + 1)
                nc.scalar.activation(std[:, :], gvar[:, :], ACT.Sqrt).then_inc(std_ready, 1)

            def split_hi(n, h):
                act.wait_ge(x_normed, n + 1)
                nc.scalar.activation(x_hi[:, h], x_raw[:, :, h * HALF:(h + 1) * HALF], ACT.Identity).then_inc(x_hi_done, 1)

            def image(i, last):
                split_hi(2 * i + 1, 1)
                for h in range(2):
                    n = 2 * i + h
                    if h == 1 and not last:
                        split_hi(2 * i + 2, 0)
                    for g in range(QK):
                        s = g % SLOTS
                        if positive(32 * (n * (QK // SLOTS) + g // SLOTS)):
                            act.wait_ge(qk_stored[s], 32 * (n * (QK // SLOTS) + g // SLOTS))
                        act.wait_ge(group_done, n * NG + g + 1)
                        nc.scalar.activation(out_hi[:, s, :], ps[:, g % BANKS, :], ACT.Identity,
                                             bias=bias[:, g:g + 1]).then_inc(hi_out, 1)
                    for g in range(VG):
                        if g == 5 and h == 0 and not last:
                            deviation(i + 1)
                        if positive(16 * (n * (VG // SLOTS) + g // SLOTS)):
                            act.wait_ge(v_stored[g % SLOTS], 16 * (n * (VG // SLOTS) + g // SLOTS))
                        act.wait_ge(group_done, n * NG + QK + g + 1)
                        nc.scalar.activation(out_v[:, g % SLOTS, :], ps[:, (QK + g) % BANKS, 0:VN],
                                             ACT.Identity).then_inc(v_out, 1)
            deviation(0)
            split_hi(0, 0)
            image(0, False)
            with act.Fori(1, B - 1) as i:
                image(i, False)
            image(B - 1, True)

        @block.vector
        def _(dve):
            dve.wait_ge(consts_in, 32)
            nc.vector.tensor_scalar(bias[:, CB:QK], bias[:, CB:QK], SCALE, None, ALU.mult).then_inc(dve_step, 1)
            for k in range(CB):
                st = w_stage[:, (k % 2) * 3 * C:(k % 2 + 1) * 3 * C]
                dve.wait_ge(w_hi_done, 3 * (k + 1))
                for cols in plain_cols:
                    nc.vector.tensor_tensor(w_lo[:, k, cols], st[:, cols], words(w_hi[:, k, cols]),
                                            ALU.subtract).then_inc(w_lo_done, 1)
                nc.vector.scalar_tensor_tensor(w_lo[:, k, k_cols], st[:, k_cols], SCALE, words(w_hi[:, k, k_cols]),
                                               ALU.mult, ALU.subtract).then_inc(w_lo_done, 1)
            STEPS = 2 * CB + 6

            def statistics(i):
                base = 1 + i * STEPS
                dve.wait_ge(x_in, 16 * (i + 1))
                for j in range(2 * CB):
                    nc.vector.bn_stats(stats[:, j, :], x_raw[:, j // 2, (j % 2) * HALF:(j % 2 + 1) * HALF]).then_inc(dve_step, 1)
                dve.wait_ge(dve_step, base + 2 * CB)
                nc.vector.memset(spread[:, :], 0.0)
                nc.vector.bn_aggr(moments[:, :], stats[:, :, :].rearrange("p a b -> p (a b)")).then_inc(part_mean, 1)

            def group_variance(i):
                base = 1 + i * STEPS + 2 * CB
                dve.wait_ge(gmean_ps, i + 1)
                nc.vector.tensor_copy(gmean[:, :], ps_stat[:, 0:2]).then_inc(dve_step, 1)
                dve.wait_ge(dve_step, base + 1)
                nc.vector.tensor_tensor(shift[:, :], moments[:, :], gmean[:, :], ALU.subtract).then_inc(dve_step, 1)
                dve.wait_ge(dve_step, base + 2)
                nc.vector.tensor_tensor(spread[:, :], shift[:, :], shift[:, :], ALU.mult).then_inc(dve_step, 1)
                dve.wait_ge(dve_step, base + 3)
                nc.vector.tensor_tensor(spread[:, 1:2], spread[:, 0:1], moments[:, 1:2], ALU.add).then_inc(part_var, 1)

            def reciprocal_deviation(i):
                base = 1 + i * STEPS + 2 * CB + 3
                dve.wait_ge(gvar_ps, i + 1)
                nc.vector.tensor_scalar(gvar[:, :], ps_stat[:, 0:2], EPS, None, ALU.add).then_inc(var_ready, 1)
                dve.wait_ge(std_ready, i + 1)
                nc.vector.reciprocal(rstd[:, :], std[:, :]).then_inc(dve_step, 3)

            def normalise(n, h, i):
                dve.wait_ge(dve_step, 1 + (i + 1) * STEPS)
                if positive((n - 1) * NG):
                    dve.wait_ge(group_done, (n - 1) * NG)
                xh = x_raw[:, :, h * HALF:(h + 1) * HALF]
                nc.vector.tensor_scalar(xh, xh, gmean[:, 0:1], rstd[:, 1:2], ALU.subtract, ALU.mult).then_inc(x_normed, 1)
                dve.wait_ge(x_hi_done, n + 1)
                nc.vector.tensor_tensor(x_lo[:, h], xh, words(x_hi[:, h]), ALU.subtract).then_inc(x_lo_done, 1)

            def image(i, last):
                normalise(2 * i + 1, 1, i)
                for h in range(2):
                    n = 2 * i + h
                    if h == 1 and not last:
                        normalise(2 * i + 2, 0, i + 1)
                    for g in range(QK):
                        s = g % SLOTS
                        if h == 0 and g == 6 and not last:
                            statistics(i + 1)
                        if h == 0 and g == 11 and not last:
                            group_variance(i + 1)
                        dve.wait_ge(hi_out, n * QK + g + 1)
                        nc.vector.scalar_tensor_tensor(out_lo[:, s, :], ps[:, g % BANKS, :], bias[:, g:g + 1],
                                                       words(out_hi[:, s, :]), ALU.add, ALU.subtract).then_inc(lo_out, 1)
                    if h == 0 and not last:
                        reciprocal_deviation(i + 1)
            statistics(0)
            group_variance(0)
            reciprocal_deviation(0)
            normalise(0, 0, 0)
            image(0, False)
            with dve.Fori(1, B - 1) as i:
                image(i, False)
            image(B - 1, True)

        @block.tensor
        def _(pe):
            def group_average(done, ready, col, i):
                pe.wait_ge(ready, i + 1)
                nc.tensor.matmul(ps_stat[:, 0:2], mean4[:, :], col, start=True, stop=True).then_inc(done, 1)

            def image(i, last):
                for h in range(2):
                    n = 2 * i + h
                    pe.wait_ge(x_lo_done, n + 1)
                    for g in range(NG):
                        if BANKS <= g < BANKS + QK:
                            pe.wait_ge(lo_out, n * QK + g - BANKS + 1)
                        else:
                            before = g - BANKS - QK if g >= BANKS else g - BANKS
                            pe.wait_ge(v_out, VG + n * VG + before + 1)
                        if g < QK:
                            out = ps[:, g % BANKS, :]
                            cols = slice(g * P, (g + 1) * P)
                            for k in range(CB):
                                a = [(w_hi, x_hi), (w_hi, x_lo), (w_lo, x_hi)]
                                for j, (w, x) in enumerate(a):
                                    last_mm = nc.tensor.matmul(out, w[:, k, cols], x[:, h, k, :],
                                                               start=(k == 0 and j == 0), stop=(k == CB - 1 and j == 2))
                        else:
                            t, c = (g - QK) // 2, (g - QK) % 2
                            out = ps[:, g % BANKS, 0:VN]
                            toks = slice(t * P, (t + 1) * P)
                            cols = slice(2 * C + c * VN, 2 * C + (c + 1) * VN)
                            for k in range(CB):
                                a = [(x_hi, w_hi), (x_hi, w_lo), (x_lo, w_hi)]
                                for j, (x, w) in enumerate(a):
                                    last_mm = nc.tensor.matmul(out, x[:, h, k, toks], w[:, k, cols],
                                                               start=(k == 0 and j == 0), stop=(k == CB - 1 and j == 2))
                        last_mm.then_inc(group_done, 1)
                        if h == 0 and not last and g == QK - 2:
                            group_average(gmean_ps, part_mean, moments[:, :], i + 1)
                        if h == 0 and not last and g == QK + 2:
                            group_average(gvar_ps, part_var, spread[:, 0:2], i + 1)
            pe.wait_ge(consts_in, 32)
            group_average(gmean_ps, part_mean, moments[:, :], 0)
            group_average(gvar_ps, part_var, spread[:, 0:2], 0)
            image(0, False)
            with pe.Fori(1, B - 1) as i:
                image(i, False)
            image(B - 1, True)


def attend(nc, qk_hi, qk_lo, v_pairs, rel_tables, one_hots, identity, rel_scratch, den_scratch, rec_scratch, o_pairs):
    q_hi_d, k_hi_d = qk_hi
    q_lo_d, k_lo_d = qk_lo
    SLOTS = 4
    with ExitStack() as ctx:
        sb = lambda name, shape, dt: ctx.enter_context(nc.sbuf_tensor(name, shape, dt))
        pb = lambda name, shape: ctx.enter_context(nc.psum_tensor(name, shape, F32))
        sem = lambda name: ctx.enter_context(nc.semaphore(name))
        two = lambda name, shape, dt: [sb(f"{name}{i}", shape, dt) for i in range(2)]
        q_hi = two("q_hi", [P, 2, T], F32R)
        q_lo = two("q_lo", [P, 2, T], F32R)
        q_max = two("q_max", [P, 2, T], F32R)
        k_hi = two("k_hi", [P, 2, T], F32R)
        k_lo = two("k_lo", [P, 2, T], F32R)
        v = two("v", [P, KB, P], F32)
        qp_hi = sb("qp_hi", [P, T], F32R)
        qp_lo = sb("qp_lo", [P, T], F32R)
        rel_hi = sb("rel_hi", [P, 2, P], F32R)
        rel_lo = sb("rel_lo", [P, 2, P], F32R)
        offs = sb("offs", [P, 2, T], F32)
        rel = sb("rel", [P, T], F32)
        prob = sb("prob", [P, 2, SLOTS, T], F32)
        prob_sum = sb("prob_sum", [P, 2, T], F32)
        raw = sb("raw", [P, T], F32)
        den = sb("den", [P, T], F32)
        den_cols = sb("den_cols", [P, 2 * T // P], F32)
        rec_cols = sb("rec_cols", [P, 2 * T // P], F32)
        rec = sb("rec", [P, T], F32)
        o = sb("o", [P, T], F32)
        ones = sb("ones", [P, D], F32)
        ident = sb("ident", [P, P], F32)
        half_max = sb("half_max", [P, 4 * KB], F32)
        mx = sb("mx", [P, P], F32)
        mx_t = sb("mx_t", [2 * KB, P], F32R)
        ps_s = pb("ps_s", [P, 2, T])
        ps_o = pb("ps_o", [P, T])
        aux = pb("aux", [P, T])
        own = [slice(0, D), slice(D, P)]
        h_rows = [slice(D, D + HS), slice(0, HS)]
        w_rows = [slice(D + HS, P), slice(HS, D)]
        max_row = [slice(D, D + 1), slice(0, 1)]

        consts_in, consts_out, memsets, table_lo = sem("consts_in"), sem("consts_out"), sem("memsets"), sem("table_lo")
        qp_in, hi_in, lo_v_in, offs_stored, rel_in, max_rows_in, o_stored = (
            sem(n) for n in ("qp_in", "hi_in", "lo_v_in", "offs_stored", "rel_in", "max_rows_in", "o_stored"))
        den_stored, den_in, rec_stored, rec_in = (sem(n) for n in ("den_stored", "den_in", "rec_stored", "rec_in"))
        offs_done, offs_out = sem("offs_done"), sem("offs_out")
        q_copied, rel_hi_done = sem("q_copied"), sem("rel_hi_done")
        rel_lo_done = [sem("rel_lo_done0"), sem("rel_lo_done1")]
        tile_done, max_done, max_ready, max_t_ps, max_t_done = (
            sem(n) for n in ("tile_done", "max_done", "max_ready", "max_t_ps", "max_t_done"))
        s_done, exp_done, pv_done = sem("s_done"), sem("exp_done"), sem("pv_done")
        sums = [sem("sum0"), sem("sum1")]
        den_done, den_out, rec_small, raw_out, o_done = (
            sem(n) for n in ("den_done", "den_out", "rec_small", "raw_out", "o_done"))
        block = ctx.enter_context(nc.Block())

        SCORES = 2 * KB
        TILES = 2 * 2 * KB
        PER_STEP = (0, 3, 5, 5, 5, 6, 6, 2)
        FIRST_TILE = [sum(PER_STEP[:kb]) for kb in range(KB)]
        MEMSETS = 7
        CONSTS_OUT = 9

        def pairs(engine, pair):
            for n in range(3):
                pair(n, n % 2)
            with engine.Fori(1, NIT // 2 - 2) as j:
                pair(2 * j + 1, 1)
                pair(2 * j + 2, 0)
            for n in range(NIT - 3, NIT):
                pair(n, n % 2)

        def rel_low(engine, n, s, e, axis):
            engine.wait_ge(rel_hi_done, 4 * n + 2 * e + 1 + axis)
            if axis == 0:
                low, raw_rows, high = q_lo[s][h_rows[e], e, :], rel[h_rows[e], :], words(q_hi[s][h_rows[e], e, :])
            else:
                low, high = (x[s][w_rows[e], e, :].rearrange("p (h w) -> p h w", w=WS) for x in (q_lo, q_hi))
                raw_rows, high = rel[w_rows[e], :].rearrange("p (w h) -> p h w", h=HS), words(high)
            engine.tensor_tensor(low, raw_rows, high, ALU.subtract).then_inc(rel_lo_done[e], 1)

        def before(n, end):
            return not isinstance(n, int) or n < end

        @block.sync
        def _(sp):
            sp.wait_ge(memsets, 1)
            for a, table in enumerate(rel_tables):
                for e in range(2):
                    sp.dma_start(offs[own[e], 0, a * P + e * D:a * P + e * D + NREL], table).then_inc(consts_in, 16)
            for e in range(2):
                sp.dma_start(rel[own[e], :], one_hots).then_inc(consts_in, 16)
            sp.dma_start(ident[:, :], identity).then_inc(consts_in, 16)

            def load_qp(n):
                sp.dma_start(words(qp_hi[:, :]), q_hi_d[n]).then_inc(qp_in, 16)
                sp.dma_start(words(qp_lo[:, :]), q_lo_d[n]).then_inc(qp_in, 16)

            def load_high(n, s):
                for e in range(2):
                    for dst, src in ((q_hi, q_hi_d), (k_hi, k_hi_d)):
                        sp.dma_start(words(dst[s][own[e], e, :]), src[n][own[e], :]).then_inc(hi_in, 16)

            def load_low(n, s):
                for dst, src in ((q_lo, q_lo_d), (k_lo, k_lo_d)):
                    for e in range(2):
                        sp.dma_start(words(dst[s][own[e], e, :]), src[n][own[e], :]).then_inc(lo_v_in, 16)

            def load_v(n, s):
                sp.dma_start(v[s][:, :, :], v_pairs[n]).then_inc(lo_v_in, 16)

            def store_offs(n, s):
                sp.wait_ge(offs_out, 4 * (n + 1))
                for a in range(2):
                    sp.dma_start(rel_scratch[s, a], offs[:, a, :]).then_inc(offs_stored, 16)

            def load_rel(n, s):
                sp.wait_ge(offs_stored, 32 * (n + 1))
                for a, rows in enumerate((h_rows, w_rows)):
                    for e in range(2):
                        src = bass.AP(rel_scratch.tensor, ((2 * s + a) * P + e * D) * T, [[T, HS], [T + WS, HS], [1, WS]])
                        sp.dma_start(rel[rows[e], :].rearrange("p (a b) -> p a b", b=WS), src).then_inc(rel_in, 16)

            def load_max_rows(n, s):
                sp.wait_ge(max_t_done, n + 1)
                for e in range(2):
                    dst = words(q_max[s][max_row[e], e, :]).rearrange("p (a b) -> p a b", b=P)
                    sp.dma_start(dst, words(mx_t[e * KB:(e + 1) * KB, :])).then_inc(max_rows_in, 16)

            def reshape_denominators(n):
                sp.wait_ge(den_out, n + 1)
                sp.dma_start(den_scratch, den[0:P:D, :]).then_inc(den_stored, 16)
                sp.wait_ge(den_stored, 16 * (n + 1))
                sp.dma_start(den_cols[:, :], den_scratch.rearrange("e (p j) -> (e p) j", j=2 * T // P)).then_inc(den_in, 16)
                sp.wait_ge(rec_small, n + 1)
                sp.dma_start(rec_scratch.rearrange("e (p j) -> (e p) j", j=2 * T // P), rec_cols[:, :]).then_inc(rec_stored, 16)
                if positive(n):
                    sp.wait_ge(o_done, n)
                sp.wait_ge(rec_stored, 16 * (n + 1))
                for e in range(2):
                    src = bass.AP(rec_scratch.tensor, e * T, [[0, D], [1, T]])
                    sp.dma_start(rec[own[e], :], src).then_inc(rec_in, 16)

            def store_o(n):
                sp.wait_ge(o_done, n + 1)
                sp.dma_start(o_pairs[n], o[:, :]).then_inc(o_stored, 16)

            load_qp(0)
            sp.wait_ge(memsets, MEMSETS)
            load_high(0, 0)
            store_offs(0, 0)
            load_qp(1)
            sp.wait_ge(consts_out, CONSTS_OUT)
            load_rel(0, 0)
            load_low(0, 0)
            load_v(0, 0)
            store_offs(1, 1)
            load_qp(2)
            for e in range(2):
                sp.wait_ge(rel_lo_done[e], 2)
            load_rel(1, 1)
            load_max_rows(0, 0)

            def pair(n, s):
                if before(n, NIT - 1):
                    if positive(SCORES * n):
                        sp.wait_ge(s_done, SCORES * n)
                    load_high(n + 1, 1 - s)
                if before(n, NIT - 2):
                    store_offs(n + 2, s)
                if before(n, NIT - 1):
                    load_low(n + 1, 1 - s)
                    if positive(KB * n):
                        sp.wait_ge(pv_done, KB * n)
                    load_v(n + 1, 1 - s)
                if positive(n):
                    reshape_denominators(n - 1)
                if before(n, NIT - 2):
                    for e in range(2):
                        sp.wait_ge(rel_lo_done[e], 2 * (n + 2))
                if before(n, NIT - 3):
                    load_qp(n + 3)
                if before(n, NIT - 2):
                    load_rel(n + 2, s)
                if positive(n):
                    store_o(n - 1)
                if before(n, NIT - 1):
                    load_max_rows(n + 1, 1 - s)
            pairs(sp, pair)
            reshape_denominators(NIT - 1)
            store_o(NIT - 1)
            sp.wait_ge(o_stored, 16 * NIT)

        @block.gpsimd
        def _(pool):
            def low_rows(n, s, axis):
                rel_low(pool, n, s, 1, axis)
                pool.wait_ge(rel_lo_done[1], 2 * n + axis + 1)

            nc.gpsimd.memset(offs[:, 0, 0:2 * P], 0.0).then_inc(memsets, 1)
            nc.gpsimd.memset(ones[:, :], 1.0).then_inc(memsets, 1)
            for s in range(2):
                nc.gpsimd.memset(words(k_lo[s][:, :, :]), 0.0).then_inc(memsets, 1)
                nc.gpsimd.memset(words(q_max[s][:, :, :]), 0.0).then_inc(memsets, 1)
            nc.gpsimd.memset(mx[:, :], 0.0).then_inc(memsets, 1)
            pool.wait_ge(memsets, MEMSETS)
            low_rows(0, 0, 0)
            low_rows(0, 0, 1)

            def pair(n, s):
                for kb in range(1, KB):
                    if kb in (4, 5) and before(n, NIT - 1):
                        pool.wait_ge(sums[0], (KB - 1) * n + kb - 1)
                        low_rows(n + 1, 1 - s, kb - 4)
                    pool.wait_ge(exp_done, SCORES * n + 2 * kb + 1)
                    if kb == 1:
                        if positive(n):
                            pool.wait_ge(den_done, n)
                        nc.gpsimd.tensor_tensor(prob_sum[:, 0, :], prob[:, 0, 0, :], prob[:, 0, 1, :], ALU.add).then_inc(sums[0], 1)
                    else:
                        pool.wait_ge(sums[0], (KB - 1) * n + kb - 1)
                        nc.gpsimd.tensor_tensor(prob_sum[:, 0, :], prob_sum[:, 0, :], prob[:, 0, kb % SLOTS, :],
                                                ALU.add).then_inc(sums[0], 1)
            pairs(pool, pair)

        @block.scalar
        def _(act):
            act.wait_ge(consts_in, 16 * 7)
            nc.scalar.activation(rel_hi[:, :, :], offs[:, 0, 0:2 * P], ACT.Identity).then_inc(consts_out, 1)
            for s in range(2):
                for e in range(2):
                    nc.scalar.activation(k_hi[s][own[1 - e], e, :], rel[own[1 - e], :], ACT.Identity).then_inc(consts_out, 1)
            act.wait_ge(memsets, MEMSETS)
            for s in range(2):
                for e in range(2):
                    nc.scalar.activation(k_lo[s][max_row[e], e, :], rel[max_row[e], :], ACT.Identity,
                                         scale=0.0, bias=1.0).then_inc(consts_out, 1)
            act.wait_ge(table_lo, 1)

            def copy_offs(n, chunks=range(4)):
                for c in chunks:
                    act.wait_ge(offs_done, 4 * n + c + 1)
                    if c == 0 and positive(n):
                        act.wait_ge(offs_stored, 32 * n)
                    nc.scalar.activation(offs[:, c // 2, (c % 2) * HALF:(c % 2 + 1) * HALF],
                                         aux[:, (c % 2) * HALF:(c % 2 + 1) * HALF], ACT.Identity).then_inc(offs_out, 1)

            def rel_high(n, s, e):
                if e == 0:
                    act.wait_ge(rel_in, 64 * (n + 1))
                nc.scalar.activation(q_hi[s][h_rows[e], e, :], rel[h_rows[e], :], ACT.Identity).then_inc(rel_hi_done, 1)
                nc.scalar.activation(q_hi[s][w_rows[e], e, :].rearrange("p (h w) -> p h w", w=WS),
                                     rel[w_rows[e], :].rearrange("p (w h) -> p h w", h=HS), ACT.Identity).then_inc(rel_hi_done, 1)

            def copy_q(n, s):
                act.wait_ge(hi_in, 16 * 4 * (n + 1))
                for e in range(2):
                    nc.scalar.activation(q_max[s][own[e], e, :], words(q_hi[s][own[e], e, :]), ACT.Identity).then_inc(q_copied, 1)

            def copy_output(n):
                act.wait_ge(pv_done, KB * (n + 1))
                if positive(n):
                    act.wait_ge(o_done, n)
                nc.scalar.activation(raw[:, :], ps_o[:, :], ACT.Identity).then_inc(raw_out, 1)

            def copy_denominators(n):
                act.wait_ge(den_done, n + 1)
                if positive(n):
                    act.wait_ge(den_stored, 16 * n)
                nc.scalar.activation(den[:, :], aux[:, :], ACT.Identity).then_inc(den_out, 1)

            copy_offs(0)
            copy_offs(1)
            rel_high(0, 0, 0)
            rel_high(0, 0, 1)
            copy_q(0, 0)

            def exp(n, kb, e):
                act.wait_ge(s_done, SCORES * n + 2 * kb + e + 1)
                if positive(KB * n + kb - SLOTS + 1):
                    act.wait_ge(pv_done, KB * n + kb - SLOTS + 1)
                    summed = max(kb - SLOTS, 1) if kb >= SLOTS else kb - SLOTS + 1
                    act.wait_ge(sums[e], (KB - 1) * n + summed)
                nc.scalar.activation(prob[:, e, kb % SLOTS, :], ps_s[:, e, :], ACT.Exp).then_inc(exp_done, 1)

            def pair(n, s):
                if before(n, NIT - 2):
                    copy_offs(n + 2, (0, 1, 2))
                for kb in range(KB):
                    exp(n, kb, 0)
                    if kb == 0 and before(n, NIT - 2):
                        copy_offs(n + 2, (3,))
                    if kb == 1 and positive(n):
                        copy_denominators(n - 1)
                    exp(n, kb, 1)
                    if kb == 0 and positive(n):
                        copy_output(n - 1)
                    if kb in (0, 2) and before(n, NIT - 1):
                        rel_high(n + 1, 1 - s, kb // 2)
                    if kb == 3 and before(n, NIT - 1):
                        copy_q(n + 1, 1 - s)
            pairs(act, pair)
            copy_output(NIT - 1)
            copy_denominators(NIT - 1)

        @block.vector
        def _(dve):
            dve.wait_ge(consts_out, 1)
            nc.vector.tensor_tensor(rel_lo[:, :, :].rearrange("p a b -> p (a b)"), offs[:, 0, 0:2 * P],
                                    words(rel_hi[:, :, :]).rearrange("p a b -> p (a b)"), ALU.subtract).then_inc(table_lo, 1)
            dve.wait_ge(memsets, MEMSETS)

            def row_max(n, t):
                dve.wait_ge(tile_done, TILES * n + t + 1)
                if t == 0 and positive(n):
                    dve.wait_ge(max_ready, n)
                nc.vector.reduce_max(half_max[:, t:t + 1], aux[:, (t % 2) * HALF:(t % 2 + 1) * HALF], AX_X).then_inc(max_done, 1)

            def negate_max(n):
                dve.wait_ge(max_done, TILES * (n + 1))
                if positive(n):
                    dve.wait_ge(max_t_ps, n)
                nc.vector.reduce_max(mx[:, 0:2 * KB], half_max[:, :].rearrange("p (t h) -> p t h", h=2), AX_X).then_inc(max_ready, 1)
                dve.wait_ge(max_t_ps, n + 1)
                if positive(n):
                    dve.wait_ge(max_rows_in, 32 * n)
                nc.vector.tensor_scalar(mx_t[:, :], aux[0:2 * KB, 0:P], -1.0, None, ALU.mult).then_inc(max_t_done, 1)

            def add(n, kb):
                dve.wait_ge(exp_done, SCORES * n + 2 * kb + 2)
                if kb == 1:
                    if positive(n):
                        dve.wait_ge(den_done, n)
                    nc.vector.tensor_tensor(prob_sum[:, 1, :], prob[:, 1, 0, :], prob[:, 1, 1, :], ALU.add).then_inc(sums[1], 1)
                else:
                    dve.wait_ge(sums[1], (KB - 1) * n + kb - 1)
                    nc.vector.tensor_tensor(prob_sum[:, 1, :], prob_sum[:, 1, :], prob[:, 1, kb % SLOTS, :],
                                            ALU.add).then_inc(sums[1], 1)

            def invert_denominators(n):
                dve.wait_ge(den_in, 16 * (n + 1))
                if positive(n):
                    dve.wait_ge(rec_stored, 16 * n)
                nc.vector.reciprocal(rec_cols[:, :], den_cols[:, :]).then_inc(rec_small, 1)

            def normalise(n):
                dve.wait_ge(rec_in, 32 * (n + 1))
                dve.wait_ge(raw_out, n + 1)
                if positive(n):
                    dve.wait_ge(o_stored, 16 * n)
                nc.vector.tensor_tensor(o[:, :], raw[:, :], rec[:, :], ALU.mult).then_inc(o_done, 1)

            rel_low(dve, 0, 0, 0, 0)
            rel_low(dve, 0, 0, 0, 1)
            for t in range(TILES):
                row_max(0, t)
            negate_max(0)

            def pair(n, s):
                for kb in range(KB):
                    if kb >= 2:
                        add(n, kb - 1)
                    elif kb == 0 and positive(n):
                        add(n - 1, KB - 1)
                    if kb == 0 and before(n, NIT - 1):
                        rel_low(dve, n + 1, 1 - s, 0, 0)
                        rel_low(dve, n + 1, 1 - s, 0, 1)
                    if before(n, NIT - 1):
                        for t in range(FIRST_TILE[kb], FIRST_TILE[kb] + PER_STEP[kb]):
                            row_max(n + 1, t)
                    if kb == 3 and positive(n):
                        invert_denominators(n - 1)
                    if kb == 5 and positive(n):
                        normalise(n - 1)
                if before(n, NIT - 1):
                    negate_max(n + 1)
            pairs(dve, pair)
            add(NIT - 1, KB - 1)
            invert_denominators(NIT - 1)
            normalise(NIT - 1)

        @block.tensor
        def _(pe):
            def offsets(n, chunks=range(4)):
                pe.wait_ge(qp_in, 32 * (n + 1))
                for c in chunks:
                    a, half = c // 2, c % 2
                    if c < 2:
                        if positive(n - 1):
                            pe.wait_ge(max_t_done, n - 1)
                        elif isinstance(n, int) and n == 1:
                            pe.wait_ge(offs_out, 4)
                    else:
                        pe.wait_ge(offs_out, 4 * n + c - 1)
                    for j, (table, q) in enumerate(((rel_hi, qp_hi), (rel_hi, qp_lo), (rel_lo, qp_hi))):
                        if a == 0:
                            moving = q[:, half * HALF:(half + 1) * HALF]
                        else:
                            moving = q[:, :].rearrange("p (h w) -> p w h", w=WS)[:, half * WS // 2:(half + 1) * WS // 2, :]
                        mm = nc.tensor.matmul(aux[:, half * HALF:(half + 1) * HALF], table[:, a, :], moving,
                                              start=(j == 0), stop=(j == 2))
                    mm.then_inc(offs_done, 1)

            def max_tile(n, s, t):
                e, qb, half = t // (2 * KB), t // 2 % KB, t % 2
                if t == 0:
                    if before(n, NIT - 1):
                        pe.wait_ge(offs_out, 4 * (n + 2))
                    if positive(n - 1):
                        pe.wait_ge(den_out, n - 1)
                    pe.wait_ge(hi_in, 16 * 4 * (n + 1))
                if t >= 2:
                    pe.wait_ge(max_done, TILES * n + t - 1)
                if t % (2 * KB) == 0:
                    pe.wait_ge(rel_hi_done, 4 * n + 2 * e + 2)
                mm = nc.tensor.matmul(aux[:, half * HALF:(half + 1) * HALF], q_hi[s][:, e, qb * P:(qb + 1) * P],
                                      k_hi[s][:, e, half * HALF:(half + 1) * HALF], start=True, stop=True)
                mm.then_inc(tile_done, 1)

            def transpose_max(n):
                pe.wait_ge(max_ready, n + 1)
                nc.tensor.transpose(aux[:, 0:P], mx[:, :], ident[:, :]).then_inc(max_t_ps, 1)

            def scores(n, s, e, kb, j):
                keys = slice(kb * P, (kb + 1) * P)
                if j == 0:
                    if kb == 0 and e == 0:
                        pe.wait_ge(lo_v_in, 16 * 5 * (n + 1))
                        for i in range(2):
                            pe.wait_ge(rel_lo_done[i], 2 * (n + 1))
                        pe.wait_ge(q_copied, 2 * (n + 1))
                    if positive(SCORES * n + 2 * (kb - 1) + e + 1):
                        pe.wait_ge(exp_done, SCORES * n + 2 * (kb - 1) + e + 1)
                if j == 2 and kb == 0 and e == 0:
                    pe.wait_ge(max_rows_in, 32 * (n + 1))
                k, q = ((k_hi, q_hi), (k_hi, q_lo), (k_lo, q_max))[j]
                for half in range(2):
                    cols = slice(half * HALF, (half + 1) * HALF)
                    mm = nc.tensor.matmul(ps_s[:, e, cols], k[s][:, e, keys], q[s][:, e, cols],
                                          start=(j == 0), stop=(j == 2))
                if j == 2:
                    mm.then_inc(s_done, 1)

            def values(n, s, kb, half):
                if half == 0:
                    pe.wait_ge(exp_done, SCORES * n + 2 * kb + 2)
                for e in range(2):
                    cols = slice(half * HALF, (half + 1) * HALF)
                    mm = nc.tensor.matmul(ps_o[own[e], cols], v[s][:, kb, own[e]], prob[:, e, kb % SLOTS, cols],
                                          start=(kb == 0), stop=(kb == KB - 1))
                if half == 1:
                    mm.then_inc(pv_done, 1)

            def denominators(n):
                if before(n, NIT - 3):
                    pe.wait_ge(offs_out, 4 * (n + 4))
                if before(n, NIT - 1):
                    pe.wait_ge(max_t_done, n + 2)
                for e in range(2):
                    pe.wait_ge(sums[e], (KB - 1) * (n + 1))
                for half in range(2):
                    for e in range(2):
                        cols = slice(half * HALF, (half + 1) * HALF)
                        mm = nc.tensor.matmul(aux[own[e], cols], ones[:, :], prob_sum[:, e, cols], start=True, stop=True)
                mm.then_inc(den_done, 1)

            pe.wait_ge(memsets, MEMSETS)
            pe.wait_ge(consts_out, CONSTS_OUT)
            pe.wait_ge(table_lo, 1)
            offsets(0)
            offsets(1)
            for t in range(TILES):
                max_tile(0, 0, t)
            transpose_max(0)

            def first_step(n, s):
                more = before(n, NIT - 2)
                if more:
                    offsets(n + 2, (0, 1))
                for e in range(2):
                    scores(n, s, e, 0, 0)
                    scores(n, s, e, 0, 1)
                for e in range(2):
                    if more:
                        offsets(n + 2, (2 + e,))
                    scores(n, s, e, 0, 2)
                if positive(n):
                    values(n - 1, 1 - s, KB - 1, 0)
                    values(n - 1, 1 - s, KB - 1, 1)

            def step(n, s, kb):
                t, last = FIRST_TILE[kb], FIRST_TILE[kb] + PER_STEP[kb] if before(n, NIT - 1) else 0

                def tile():
                    nonlocal t
                    if t < last:
                        max_tile(n + 1, 1 - s, t)
                        t += 1
                for e in range(2):
                    for j in range(3):
                        if (3 * e + j) % 2 == 0 and kb > 1:
                            tile()
                        scores(n, s, e, kb, j)
                    if e == 0 and kb == 1 and positive(n):
                        denominators(n - 1)
                if kb == 1 and positive(n):
                    pe.wait_ge(raw_out, n)
                tile()
                values(n, s, kb - 1, 0)
                if kb == KB - 1 and before(n, NIT - 1):
                    transpose_max(n + 1)
                tile()
                values(n, s, kb - 1, 1)
                tile()

            def pair(n, s):
                first_step(n, s)
                for kb in range(1, KB):
                    step(n, s, kb)
            pairs(pe, pair)
            values(NIT - 1, 1, KB - 1, 0)
            values(NIT - 1, 1, KB - 1, 1)
            denominators(NIT - 1)


def project_out(nc, x_t, o_pairs, w_t, v_bias_cols, bias_cols, out_t):
    with ExitStack() as ctx:
        sb = lambda name, shape, dt: ctx.enter_context(nc.sbuf_tensor(name, shape, dt))
        sem = lambda name: ctx.enter_context(nc.semaphore(name))
        w_raw = sb("w_raw", [P, CB, C], F32)
        w_hi = sb("wp_hi", [P, CB, C], F32R)
        w_lo = sb("wp_lo", [P, CB, C], F32R)
        o_raw = sb("o_raw", [P, 2, CB, HALF], F32)
        o_hi = sb("o_hi", [P, 2, CB, HALF], F32R)
        o_lo = sb("o_lo", [P, 2, CB, HALF], F32R)
        x_res = sb("x_res", [P, 2, CB, HALF], F32)
        y = sb("y", [P, CB, HALF], F32)
        v_bias = sb("o_bias", [P, CB], F32)
        bias = sb("p_bias", [P, CB], F32)
        ps = ctx.enter_context(nc.psum_tensor("ps_y", [P, CB, HALF], F32))
        w_in, w_hi_done, w_lo_done, bias_in = sem("wp_in"), sem("wp_hi_done"), sem("wp_lo_done"), sem("p3_bias_in")
        o_in = [sem(f"o_in{i}") for i in range(2)]
        x_in = [sem(f"res_in{i}") for i in range(2)]
        o_hi_done, o_lo_done = sem("o_hi_done"), sem("o_lo_done")
        block_done, y_done = sem("block_done"), sem("y_done")
        y_stored = [sem(f"y_stored{i}") for i in range(CB)]
        block = ctx.enter_context(nc.Block())

        @block.sync
        def _(sp):
            sp.dma_start(v_bias[:, :], v_bias_cols).then_inc(bias_in, 16)
            sp.dma_start(bias[:, :], bias_cols).then_inc(bias_in, 16)
            sp.dma_start(w_raw[:, :, :], w_t.rearrange("(k p) n -> p k n", p=P)).then_inc(w_in, 16)

            def load(i, h):
                cols = slice(h * HALF, (h + 1) * HALF)
                sp.dma_start(o_raw[:, h], o_pairs[i].rearrange("j p t -> p j t")[:, :, cols]).then_inc(o_in[h], 16)
                sp.dma_start(x_res[:, h], x_t[i].rearrange("(k p) t -> p k t", p=P)[:, :, cols]).then_inc(x_in[h], 16)

            load(0, 0)
            load(0, 1)

            def image(i, last):
                for h in range(2):
                    n = 2 * i + h
                    for g in range(CB):
                        sp.wait_ge(y_done, n * CB + g + 1)
                        sp.dma_start(out_t[i, g * P:(g + 1) * P, h * HALF:(h + 1) * HALF], y[:, g, :]).then_inc(y_stored[g], 16)
                    if not last:
                        sp.wait_ge(o_lo_done, n + 1)
                        load(i + 1, h)
            image(0, False)
            with sp.Fori(1, B - 1) as i:
                image(i, False)
            image(B - 1, True)
            for g in range(CB):
                sp.wait_ge(y_stored[g], 16 * 2 * B)

        @block.scalar
        def _(act):
            act.wait_ge(w_in, 16)
            nc.scalar.activation(w_hi[:, :, :], w_raw[:, :, :], ACT.Identity).then_inc(w_hi_done, 1)
            act.wait_ge(bias_in, 32)

            def split_hi(i, h, n):
                act.wait_ge(o_in[h], 16 * (i + 1))
                if not (isinstance(n, int) and n < 2):
                    act.wait_ge(block_done, (n - 1) * CB)
                for k in range(CB):
                    nc.scalar.activation(o_hi[:, h, k, :], o_raw[:, h, k, :], ACT.Identity,
                                         bias=v_bias[:, k:k + 1]).then_inc(o_hi_done, 1)
            split_hi(0, 0, 0)
            split_hi(0, 1, 1)
            with act.Fori(0, B - 1) as i:
                for h in range(2):
                    split_hi(i + 1, h, 2 * i + 2 + h)

        @block.vector
        def _(dve):
            dve.wait_ge(w_hi_done, 1)
            nc.vector.tensor_tensor(w_lo[:, :, :], w_raw[:, :, :], words(w_hi[:, :, :]), ALU.subtract).then_inc(w_lo_done, 1)
            dve.wait_ge(bias_in, 32)

            def split_lo(n, h):
                for k in range(CB):
                    dve.wait_ge(o_hi_done, n * CB + k + 1)
                    op = nc.vector.scalar_tensor_tensor(o_lo[:, h, k, :], o_raw[:, h, k, :], v_bias[:, k:k + 1],
                                                        words(o_hi[:, h, k, :]), ALU.add, ALU.subtract)
                op.then_inc(o_lo_done, 1)

            def finish(i, n, h):
                for g in range(CB):
                    dve.wait_ge(block_done, n * CB + g + 1)
                    if g == 0:
                        dve.wait_ge(x_in[h], 16 * (i + 1))
                    if positive(16 * n):
                        dve.wait_ge(y_stored[g], 16 * n)
                    nc.vector.scalar_tensor_tensor(y[:, g, :], ps[:, g, :], bias[:, g:g + 1], x_res[:, h, g, :],
                                                   ALU.add, ALU.add).then_inc(y_done, 1)
            split_lo(0, 0)
            split_lo(1, 1)

            def image(i):
                for h in range(2):
                    finish(i, 2 * i + h, h)
                    split_lo(2 * i + h + 2, h)
            image(0)
            with dve.Fori(1, B - 1) as i:
                image(i)
            for h in range(2):
                finish(B - 1, 2 * (B - 1) + h, h)

        @block.tensor
        def _(pe):
            pe.wait_ge(w_lo_done, 1)

            def image(i, first):
                for h in range(2):
                    n = 2 * i + h
                    pe.wait_ge(o_lo_done, n + 1)
                    for g in range(CB):
                        if not (first and h == 0):
                            pe.wait_ge(y_done, (n - 1) * CB + g + 1)
                        cols = slice(g * P, (g + 1) * P)
                        for k in range(CB):
                            for j, (w, o) in enumerate(((w_hi, o_hi), (w_hi, o_lo), (w_lo, o_hi))):
                                mm = nc.tensor.matmul(ps[:, g, :], w[:, k, cols], o[:, h, k, :],
                                                      start=(k == 0 and j == 0), stop=(k == CB - 1 and j == 2))
                        mm.then_inc(block_done, 1)
            image(0, True)
            with pe.Fori(1, B) as i:
                image(i, False)


def build(nc, io):
    scratch = lambda name, shape: nc.dram_tensor(name, shape, F32, kind="Internal").ap()
    qk_hi = [scratch(f"{n}_hi_d", (NIT, P, T)) for n in "qk"]
    qk_lo = [scratch(f"{n}_lo_d", (NIT, P, T)) for n in "qk"]
    v_d = scratch("v_d", (NIT, P, KB, P))
    rel_scratch = scratch("rel_d", (2, 2, P, T))
    den_scratch, rec_scratch = scratch("den_d", (2, T)), scratch("rec_d", (2, T))
    o_d = scratch("o_d", (NIT, P, T))
    by_image = lambda ap: ap.rearrange("(i j) p t -> i (j p) t", j=NPAIR)
    project_qkv(nc, io["x_t"], io["qkv_w_t"], io["qk_bias"], io["group_mean"],
                [by_image(a) for a in qk_hi], [by_image(a) for a in qk_lo],
                v_d.rearrange("(i j) p k d -> i j p k d", j=NPAIR))
    attend(nc, qk_hi, qk_lo, v_d, (io["rel_h_t"], io["rel_w_t"]), io["one_hots"], io["identity"], rel_scratch,
           den_scratch, rec_scratch, o_d)
    project_out(nc, io["x_t"], o_d.rearrange("(i j) p t -> i j p t", j=NPAIR), io["proj_w_t"], io["v_bias"],
                io["proj_bias"], io["out_t"])


def shape_constants():
    q = np.arange(P) // PER_GROUP
    token = np.arange(T)
    j = np.arange(HS)[:, None]
    return {
        "group_mean": (q[:, None] == q[None, :]).astype(np.float32) / PER_GROUP,
        "one_hots": np.concatenate([HS - 1 - j == token // WS, WS - 1 - j == token % WS]).astype(np.float32),
        "identity": np.eye(P, dtype=np.float32),
    }


def kernel(x, L0_conv_qkv_w, L0_conv_qkv_b, L0_conv_proj_w, L0_conv_proj_b, L0_conv_rel_pos_h, L0_conv_rel_pos_w):
    import concourse.bacc as bacc
    from concourse.bass_utils import run_bass_kernel_spmd

    cols = lambda v: np.ascontiguousarray(np.asarray(v).reshape(-1, P).T)
    qkv_b = np.asarray(L0_conv_qkv_b)
    arrays = {
        "x_t": np.ascontiguousarray(np.asarray(x).reshape(B, T, C).transpose(0, 2, 1)),
        "qkv_w_t": np.ascontiguousarray(np.asarray(L0_conv_qkv_w).T),
        "proj_w_t": np.ascontiguousarray(np.asarray(L0_conv_proj_w).T),
        "qk_bias": cols(qkv_b[:2 * C]),
        "v_bias": cols(qkv_b[2 * C:]),
        "proj_bias": cols(L0_conv_proj_b),
        "rel_h_t": np.ascontiguousarray(np.asarray(L0_conv_rel_pos_h).T),
        "rel_w_t": np.ascontiguousarray(np.asarray(L0_conv_rel_pos_w).T),
        **shape_constants(),
    }
    nc = bacc.Bacc("TRN2", target_bir_lowering=False, num_devices=1)
    io = {n: nc.dram_tensor(n, a.shape, F32, kind="ExternalInput").ap() for n, a in arrays.items()}
    io["out_t"] = nc.dram_tensor("out_t", (B, C, T), F32, kind="ExternalOutput").ap()
    build(nc, io)
    result = run_bass_kernel_spmd(nc, [arrays], core_ids=[0])
    out = result.results[0]["out_t"]
    return np.ascontiguousarray(out.transpose(0, 2, 1)).reshape(B, HS, WS, C)
```

```python
from contextlib import ExitStack

import numpy as np
import concourse.bass as bass
from concourse import mybir

F32 = mybir.dt.float32
F32R = mybir.dt.float32r
ACT = mybir.ActivationFunctionType
ALU = mybir.AluOpType
AX_X = mybir.AxisListType.X

P = 128
B, HS, WS, C = 8, 32, 32, 768
T = HS * WS
HALF = T // 2
NH, D = 12, 64
NPAIR = NH // 2
NIT = B * NPAIR
CB = C // P
KB = T // P
NREL = 2 * HS - 1
GROUP = C // 32
PER_GROUP = GROUP // CB
EPS = 1e-5
SCALE = float(D) ** -0.5


def positive(value):
    return not isinstance(value, int) or value > 0


def words(ap):
    return ap.bitcast(F32)


def project_qkv(nc, x_t, w_t, bias_cols, group_mean, qk_hi, qk_lo, v_rows):
    QK = 2 * CB
    VN = C // 2
    VG = 2 * (HALF // P)
    NG = QK + VG
    BANKS, SLOTS = 5, 4
    with ExitStack() as ctx:
        sb = lambda name, shape, dt: ctx.enter_context(nc.sbuf_tensor(name, shape, dt))
        sem = lambda name: ctx.enter_context(nc.semaphore(name))
        w_hi = sb("w_hi", [P, CB, 3 * C], F32R)
        w_lo = sb("w_lo", [P, CB, 3 * C], F32R)
        x_hi = sb("x_hi", [P, 2, CB, HALF], F32R)
        x_lo = sb("x_lo", [P, 2, CB, HALF], F32R)
        x_raw = sb("x_raw", [P, CB, T], F32)
        out_slots = sb("out_slots", [P, SLOTS * (2 * HALF + VN)], F32)
        out_hi, out_lo = (out_slots[:, i * SLOTS * HALF:(i + 1) * SLOTS * HALF].rearrange("p (s t) -> p s t", s=SLOTS) for i in range(2))
        out_v = out_slots[:, 2 * SLOTS * HALF:].rearrange("p (s t) -> p s t", s=SLOTS)
        W_PART = 2 * C
        w_stage = [out_slots[:, i * W_PART:(i + 1) * W_PART].rearrange("p (k n) -> p k n", k=2) for i in range(3)]
        bias = sb("bias", [P, QK], F32)
        mean4 = sb("mean4", [P, P], F32)
        stats = sb("stats", [P, 2 * CB, 6], F32)
        moments = sb("moments", [P, 2], F32)
        gmean = sb("gmean", [P, 2], F32)
        shift = sb("shift", [P, 2], F32)
        spread = sb("spread", [P, 2], F32)
        gvar = sb("gvar", [P, 2], F32)
        std = sb("std", [P, 2], F32)
        rstd = sb("rstd", [P, 2], F32)
        ps = ctx.enter_context(nc.psum_tensor("ps_qkv", [P, BANKS, HALF], F32))
        ps_stat = ctx.enter_context(nc.psum_tensor("ps_stat", [P, HALF], F32))
        consts_in = sem("p1_consts_in")
        w_in = [sem(f"w_in{i}") for i in range(3)]
        w_hi_done = sem("w_hi_done")
        w_lo_done = [sem(f"w_lo_done{i}") for i in range(3)]
        x0_in = [sem(f"x0_in{i}") for i in range(2)]
        x_in = sem("x_in")
        dve_step = sem("dve_step")
        part_mean, gmean_ps, part_var, gvar_ps = sem("part_mean"), sem("gmean_ps"), sem("part_var"), sem("gvar_ps")
        var_ready, std_ready = sem("var_ready"), sem("std_ready")
        x_normed, x_hi_done, x_lo_done = sem("x_normed"), sem("x_hi_done"), sem("x_lo_done")
        group_done = sem("group_done")
        hi_out, lo_out = sem("hi_out"), sem("lo_out")
        v_out = sem("v_out")
        qk_stored = [sem(f"qk_stored{i}") for i in range(SLOTS)]
        v_stored = [sem(f"v_stored{i}") for i in range(SLOTS)]
        block = ctx.enter_context(nc.Block())
        W_PARTS = 3 * CB // 2

        def w_part(tensor, c):
            return tensor[:, 2 * (c // 3):2 * (c // 3) + 2, (c % 3) * C:(c % 3 + 1) * C]

        def w_on_pool(c):
            return c in (2, 5, 6)

        @block.sync
        def _(sp):
            sp.dma_start(bias[:, :], bias_cols).then_inc(consts_in, 16)
            sp.dma_start(mean4[:, :], group_mean).then_inc(consts_in, 16)
            x0 = x_t[0].rearrange("(p k) t -> p k t", k=CB)
            for c in range(2):
                ks = slice(c * CB // 2, (c + 1) * CB // 2)
                sp.dma_start(x_raw[:, ks, :], x0[:, ks, :]).then_inc(x0_in[c], 16)
            w_rows = w_t.rearrange("(p k) n -> p k n", k=CB)
            for c in range(W_PARTS):
                if c >= 3:
                    sp.wait_ge(w_lo_done[c % 3], c // 3)
                sp.dma_start(w_stage[c % 3], w_part(w_rows, c)).then_inc(w_in[c % 3], 16)

            def image(i, last):
                for h in range(2):
                    n = 2 * i + h
                    for g in range(QK):
                        sp.wait_ge(lo_out, n * QK + g + 1)
                        rows = slice((g % CB) * P, (g % CB + 1) * P)
                        cols = slice(h * HALF, (h + 1) * HALF)
                        s = g % SLOTS
                        sp.dma_start(qk_hi[g // CB][i, rows, cols], out_hi[:, s, :]).then_inc(qk_stored[s], 16)
                        sp.dma_start(qk_lo[g // CB][i, rows, cols], out_lo[:, s, :]).then_inc(qk_stored[s], 16)
                        if h == 0 and g == 1 and not last:
                            sp.wait_ge(x_lo_done, 2 * i + 2)
                            sp.dma_start(x_raw[:, :, :], x_t[i + 1].rearrange("(p k) t -> p k t", k=CB)).then_inc(x_in, 16)
                    for g in range(VG):
                        sp.wait_ge(v_out, VG + n * VG + g + 1)
                        kb, c = h * (HALF // P) + g // 2, g % 2
                        dst = v_rows[i, c * (NPAIR // 2):(c + 1) * (NPAIR // 2), :, kb, :].rearrange("j p d -> p j d")
                        sp.dma_start(dst, out_v[:, g % SLOTS, :].rearrange("p (j d) -> p j d", d=P)).then_inc(v_stored[g % SLOTS], 16)
            image(0, False)
            with sp.Fori(1, B - 1) as i:
                image(i, False)
            image(B - 1, True)
            for s in range(SLOTS):
                sp.wait_ge(qk_stored[s], 32 * 2 * B * QK // SLOTS)
                sp.wait_ge(v_stored[s], 16 * 2 * B * VG // SLOTS)

        @block.scalar
        def _(act):
            act.sem_inc(v_out, VG)

            def deviation(i):
                act.wait_ge(var_ready, i + 1)
                nc.scalar.activation(std[:, :], gvar[:, :], ACT.Sqrt).then_inc(std_ready, 1)

            def split_hi(n, h):
                act.wait_ge(x_normed, n + 1)
                nc.scalar.activation(x_hi[:, h], x_raw[:, :, h * HALF:(h + 1) * HALF], ACT.Identity).then_inc(x_hi_done, 1)

            def image(i, last):
                split_hi(2 * i + 1, 1)
                for h in range(2):
                    n = 2 * i + h
                    if h == 1 and not last:
                        split_hi(2 * i + 2, 0)
                    for g in range(QK):
                        s = g % SLOTS
                        if positive(32 * (n * (QK // SLOTS) + g // SLOTS)):
                            act.wait_ge(qk_stored[s], 32 * (n * (QK // SLOTS) + g // SLOTS))
                        act.wait_ge(group_done, n * NG + g + 1)
                        nc.scalar.activation(out_hi[:, s, :].bitcast(F32R), ps[:, g % BANKS, :], ACT.Identity,
                                             bias=bias[:, g:g + 1]).then_inc(hi_out, 1)
                    for g in range(VG):
                        if g == 5 and h == 0 and not last:
                            deviation(i + 1)
                        if positive(16 * (n * (VG // SLOTS) + g // SLOTS)):
                            act.wait_ge(v_stored[g % SLOTS], 16 * (n * (VG // SLOTS) + g // SLOTS))
                        act.wait_ge(group_done, n * NG + QK + g + 1)
                        nc.scalar.activation(out_v[:, g % SLOTS, :], ps[:, (QK + g) % BANKS, 0:VN],
                                             ACT.Identity).then_inc(v_out, 1)
            for c in range(W_PARTS):
                act.wait_ge(w_in[c % 3], 16 * (c // 3 + 1))
                nc.scalar.activation(w_part(w_hi, c), w_stage[c % 3], ACT.Identity,
                                     scale=SCALE if c % 3 == 1 else 1.0).then_inc(w_hi_done, 1)
                if c == 4:
                    deviation(0)
                if c == 7:
                    split_hi(0, 0)
            image(0, False)
            with act.Fori(1, B - 1) as i:
                image(i, False)
            image(B - 1, True)

        @block.gpsimd
        def _(pool):
            for c in filter(w_on_pool, range(W_PARTS)):
                pool.wait_ge(w_hi_done, c + 1)
                nc.gpsimd.tensor_tensor(w_part(w_lo, c), w_stage[c % 3], words(w_part(w_hi, c)),
                                        ALU.subtract).then_inc(w_lo_done[c % 3], 1)

        @block.vector
        def _(dve):
            dve.wait_ge(consts_in, 32)
            nc.vector.tensor_scalar(bias[:, CB:QK], bias[:, CB:QK], SCALE, None, ALU.mult).then_inc(dve_step, 1)

            def split_w_lo(parts):
                for c in parts:
                    dve.wait_ge(w_hi_done, c + 1)
                    nc.vector.scalar_tensor_tensor(w_part(w_lo, c), w_stage[c % 3], SCALE if c % 3 == 1 else 1.0,
                                                   words(w_part(w_hi, c)), ALU.mult, ALU.subtract).then_inc(w_lo_done[c % 3], 1)

            STEPS = 2 * CB + 6

            def statistics(i):
                base = 1 + i * STEPS
                first = isinstance(i, int) and i == 0
                if not first:
                    dve.wait_ge(x_in, 16 * i)
                for j in range(2 * CB):
                    if first and j % CB == 0:
                        dve.wait_ge(x0_in[j // CB], 16)
                    nc.vector.bn_stats(stats[:, j, :], x_raw[:, j // 2, (j % 2) * HALF:(j % 2 + 1) * HALF]).then_inc(dve_step, 1)
                dve.wait_ge(dve_step, base + 2 * CB)
                nc.vector.memset(spread[:, :], 0.0)
                nc.vector.bn_aggr(moments[:, :], stats[:, :, :].rearrange("p a b -> p (a b)")).then_inc(part_mean, 1)

            def group_variance(i):
                base = 1 + i * STEPS + 2 * CB
                dve.wait_ge(gmean_ps, i + 1)
                nc.vector.tensor_copy(gmean[:, :], ps_stat[:, 0:2]).then_inc(dve_step, 1)
                dve.wait_ge(dve_step, base + 1)
                nc.vector.tensor_tensor(shift[:, :], moments[:, :], gmean[:, :], ALU.subtract).then_inc(dve_step, 1)
                dve.wait_ge(dve_step, base + 2)
                nc.vector.tensor_tensor(spread[:, :], shift[:, :], shift[:, :], ALU.mult).then_inc(dve_step, 1)
                dve.wait_ge(dve_step, base + 3)
                nc.vector.tensor_tensor(spread[:, 1:2], spread[:, 0:1], moments[:, 1:2], ALU.add).then_inc(part_var, 1)

            def reciprocal_deviation(i):
                base = 1 + i * STEPS + 2 * CB + 3
                dve.wait_ge(gvar_ps, i + 1)
                nc.vector.tensor_scalar(gvar[:, :], ps_stat[:, 0:2], EPS, None, ALU.add).then_inc(var_ready, 1)
                dve.wait_ge(std_ready, i + 1)
                nc.vector.reciprocal(rstd[:, :], std[:, :]).then_inc(dve_step, 3)

            def normalise(n, h, i):
                dve.wait_ge(dve_step, 1 + (i + 1) * STEPS)
                if positive((n - 1) * NG):
                    dve.wait_ge(group_done, (n - 1) * NG)
                xh = x_raw[:, :, h * HALF:(h + 1) * HALF]
                nc.vector.tensor_scalar(xh, xh, gmean[:, 0:1], rstd[:, 1:2], ALU.subtract, ALU.mult).then_inc(x_normed, 1)
                dve.wait_ge(x_hi_done, n + 1)
                nc.vector.tensor_tensor(x_lo[:, h], xh, words(x_hi[:, h]), ALU.subtract).then_inc(x_lo_done, 1)

            def image(i, last):
                normalise(2 * i + 1, 1, i)
                for h in range(2):
                    n = 2 * i + h
                    if h == 1 and not last:
                        normalise(2 * i + 2, 0, i + 1)
                    for g in range(QK):
                        s = g % SLOTS
                        if h == 0 and g == 6 and not last:
                            statistics(i + 1)
                        if h == 0 and g == 11 and not last:
                            group_variance(i + 1)
                        dve.wait_ge(hi_out, n * QK + g + 1)
                        nc.vector.scalar_tensor_tensor(out_lo[:, s, :].bitcast(F32R), ps[:, g % BANKS, :], bias[:, g:g + 1],
                                                       out_hi[:, s, :], ALU.add, ALU.subtract).then_inc(lo_out, 1)
                    if h == 0 and not last:
                        reciprocal_deviation(i + 1)
            statistics(0)
            split_w_lo((0, 1))
            group_variance(0)
            split_w_lo((3,))
            reciprocal_deviation(0)
            split_w_lo((4,))
            normalise(0, 0, 0)
            split_w_lo((7, 8))
            image(0, False)
            with dve.Fori(1, B - 1) as i:
                image(i, False)
            image(B - 1, True)

        @block.tensor
        def _(pe):
            def group_average(done, ready, col, i):
                pe.wait_ge(ready, i + 1)
                nc.tensor.matmul(ps_stat[:, 0:2], mean4[:, :], col, start=True, stop=True).then_inc(done, 1)

            def image(i, last):
                for h in range(2):
                    n = 2 * i + h
                    pe.wait_ge(x_lo_done, n + 1)
                    for g in range(NG):
                        if BANKS <= g < BANKS + QK:
                            pe.wait_ge(lo_out, n * QK + g - BANKS + 1)
                        else:
                            before = g - BANKS - QK if g >= BANKS else g - BANKS
                            pe.wait_ge(v_out, VG + n * VG + before + 1)
                        if g < QK:
                            out = ps[:, g % BANKS, :]
                            cols = slice(g * P, (g + 1) * P)
                            for k in range(CB):
                                a = [(w_hi, x_hi), (w_hi, x_lo), (w_lo, x_hi)]
                                for j, (w, x) in enumerate(a):
                                    last_mm = nc.tensor.matmul(out, w[:, k, cols], x[:, h, k, :],
                                                               start=(k == 0 and j == 0), stop=(k == CB - 1 and j == 2))
                        else:
                            t, c = (g - QK) // 2, (g - QK) % 2
                            out = ps[:, g % BANKS, 0:VN]
                            toks = slice(t * P, (t + 1) * P)
                            cols = slice(2 * C + c * VN, 2 * C + (c + 1) * VN)
                            for k in range(CB):
                                a = [(x_hi, w_hi), (x_hi, w_lo), (x_lo, w_hi)]
                                for j, (x, w) in enumerate(a):
                                    last_mm = nc.tensor.matmul(out, x[:, h, k, toks], w[:, k, cols],
                                                               start=(k == 0 and j == 0), stop=(k == CB - 1 and j == 2))
                        last_mm.then_inc(group_done, 1)
                        if h == 0 and not last and g == QK - 2:
                            group_average(gmean_ps, part_mean, moments[:, :], i + 1)
                        if h == 0 and not last and g == QK + 2:
                            group_average(gvar_ps, part_var, spread[:, 0:2], i + 1)
            pe.wait_ge(consts_in, 32)
            group_average(gmean_ps, part_mean, moments[:, :], 0)
            group_average(gvar_ps, part_var, spread[:, 0:2], 0)
            for i in range(3):
                pe.wait_ge(w_lo_done[i], 3)
            image(0, False)
            with pe.Fori(1, B - 1) as i:
                image(i, False)
            image(B - 1, True)


def attend(nc, qk_hi, qk_lo, v_pairs, rel_tables, one_hots, identity, rel_scratch, den_scratch, rec_scratch, o_pairs,
           proj_w_t, wp_hi, wp_lo):
    q_hi_d, k_hi_d = qk_hi
    q_lo_d, k_lo_d = qk_lo
    SLOTS = 4
    with ExitStack() as ctx:
        sb = lambda name, shape, dt: ctx.enter_context(nc.sbuf_tensor(name, shape, dt))
        pb = lambda name, shape: ctx.enter_context(nc.psum_tensor(name, shape, F32))
        sem = lambda name: ctx.enter_context(nc.semaphore(name))
        two = lambda name, shape, dt: [sb(f"{name}{i}", shape, dt) for i in range(2)]
        q_hi = two("q_hi", [P, 2, T], F32R)
        q_lo = two("q_lo", [P, 2, T], F32R)
        q_max = two("q_max", [P, 2, T], F32R)
        k_hi = two("k_hi", [P, 2, T], F32R)
        k_lo = two("k_lo", [P, 2, T], F32R)
        v = two("v", [P, KB, P], F32)
        qp = sb("qp", [P, 2, T], F32R)
        table_hi = sb("table_hi", [P, P], F32R)
        table_lo = sb("table_lo", [P, P], F32R)
        offs = sb("offs", [P, 2, T], F32)
        rel = sb("rel", [P, T], F32)
        prob = sb("prob", [P, 2, SLOTS, T], F32)
        prob_sum = sb("prob_sum", [P, 2, T], F32)
        raw = sb("raw", [P, T], F32)
        den = sb("den", [P, T], F32)
        den_cols = sb("den_cols", [P, 2 * T // P], F32)
        rec_cols = sb("rec_cols", [P, 2 * T // P], F32)
        rec = sb("rec", [P, T], F32)
        o = sb("o", [P, T], F32)
        ones = sb("ones", [P, D], F32)
        ident = sb("ident", [P, P], F32)
        half_max = sb("half_max", [P, 4 * KB], F32)
        mx = sb("mx", [P, P], F32)
        mx_t = sb("mx_t", [2 * KB, P], F32R)
        ps_s = pb("ps_s", [P, 2, T])
        ps_o = pb("ps_o", [P, T])
        aux = pb("aux", [P, T])
        own = [slice(0, D), slice(D, P)]
        h_rows = [slice(D, D + HS), slice(0, HS)]
        w_rows = [slice(D + HS, P), slice(HS, D)]
        max_row = [slice(D, D + 1), slice(0, 1)]

        consts_in, consts_out, memsets, tables_done = sem("consts_in"), sem("consts_out"), sem("memsets"), sem("tables_done")
        qp_in, hi_in, lo_v_in, offs_stored, rel_in, max_rows_in, o_stored = (
            sem(n) for n in ("qp_in", "hi_in", "lo_v_in", "offs_stored", "rel_in", "max_rows_in", "o_stored"))
        den_stored, den_in, rec_stored, rec_in = (sem(n) for n in ("den_stored", "den_in", "rec_stored", "rec_in"))
        offs_done, offs_out = sem("offs_done"), sem("offs_out")
        q_copied = sem("q_copied")
        rel_hi_done = [sem("rel_hi_done0"), sem("rel_hi_done1")]
        rel_lo_done = [sem("rel_lo_done0"), sem("rel_lo_done1")]
        tile_done, max_done, max_ready, max_t_ps, max_t_done = (
            sem(n) for n in ("tile_done", "max_done", "max_ready", "max_t_ps", "max_t_done"))
        wp_raw = sb("wp_raw", [P, C], F32)
        wp_in, wp_hi_done, wp_lo_done = sem("wp_in"), sem("wp_hi_done"), sem("wp_lo_done")
        wp_part = {n: k for k, n in enumerate((0, 1, 2, NIT - 3, NIT - 2, NIT - 1))}
        s_done, exp_done, pv_done = sem("s_done"), sem("exp_done"), sem("pv_done")
        sums = [sem("sum0"), sem("sum1")]
        den_done, den_out, rec_small, raw_out, o_done = (
            sem(n) for n in ("den_done", "den_out", "rec_small", "raw_out", "o_done"))
        block = ctx.enter_context(nc.Block())

        SCORES = 2 * KB
        TILES = 2 * 2 * KB
        PER_STEP = (0, 1, 6, 5, 5, 5, 5, 5)
        FIRST_TILE = [sum(PER_STEP[:kb]) for kb in range(KB)]
        MEMSETS = 7
        CONSTS_OUT = 9

        def pairs(engine, pair):
            for n in range(3):
                pair(n, n % 2)
            with engine.Fori(1, NIT // 2 - 2) as j:
                pair(2 * j + 1, 1)
                pair(2 * j + 2, 0)
            for n in range(NIT - 3, NIT):
                pair(n, n % 2)

        def rel_rows(n, s, e, axis):
            if axis == 0:
                return rel[h_rows[e], :], q_hi[s][h_rows[e], e, :], q_lo[s][h_rows[e], e, :]
            high, low = (x[s][w_rows[e], e, :].rearrange("p (h w) -> p h w", w=WS) for x in (q_hi, q_lo))
            return rel[w_rows[e], :].rearrange("p (w h) -> p h w", h=HS), high, low

        def rel_low(engine, n, s, e, axis):
            raw_rows, high, low = rel_rows(n, s, e, axis)
            engine.wait_ge(rel_hi_done[e], 2 * n + axis + 1)
            engine.tensor_tensor(low, raw_rows, words(high), ALU.subtract).then_inc(rel_lo_done[e], 1)

        def before(n, end):
            return not isinstance(n, int) or n < end

        @block.sync
        def _(sp):
            sp.wait_ge(memsets, 1)
            for a, table in enumerate(rel_tables):
                for e in range(2):
                    sp.dma_start(offs[own[e], 0, a * D:a * D + NREL], table).then_inc(consts_in, 16)
            for e in range(2):
                sp.dma_start(rel[own[e], :], one_hots).then_inc(consts_in, 16)
            sp.dma_start(ident[:, :], identity).then_inc(consts_in, 16)

            def load_qp(n):
                for part, src in enumerate((q_hi_d, q_lo_d)):
                    sp.dma_start(words(qp[own[part], :, :]), src[n].rearrange("(e p) t -> p e t", e=2)).then_inc(qp_in, 16)

            def load_high(n, s):
                for e in range(2):
                    for dst, src in ((q_hi, q_hi_d), (k_hi, k_hi_d)):
                        sp.dma_start(words(dst[s][own[e], e, :]), src[n][own[e], :]).then_inc(hi_in, 16)

            def load_low(n, s):
                for dst, src in ((q_lo, q_lo_d), (k_lo, k_lo_d)):
                    for e in range(2):
                        sp.dma_start(words(dst[s][own[e], e, :]), src[n][own[e], :]).then_inc(lo_v_in, 16)

            def load_v(n, s):
                sp.dma_start(v[s][:, :, :], v_pairs[n]).then_inc(lo_v_in, 16)

            def store_offs(n, s):
                for e in range(2):
                    sp.wait_ge(offs_out, 8 * n + 4 * (e + 1))
                    sp.dma_start(rel_scratch[s, e], offs[:, e, :]).then_inc(offs_stored, 16)

            def load_rel(n, s):
                sp.wait_ge(offs_stored, 32 * (n + 1))
                for a, rows in enumerate((h_rows, w_rows)):
                    for e in range(2):
                        src = bass.AP(rel_scratch.tensor, ((2 * s + e) * P + a * D) * T, [[T, HS], [T + WS, HS], [1, WS]])
                        sp.dma_start(rel[rows[e], :].rearrange("p (a b) -> p a b", b=WS), src).then_inc(rel_in, 16)

            def load_max_rows(n, s):
                sp.wait_ge(max_t_done, n + 1)
                for e in range(2):
                    dst = words(q_max[s][max_row[e], e, :]).rearrange("p (a b) -> p a b", b=P)
                    sp.dma_start(dst, words(mx_t[e * KB:(e + 1) * KB, :])).then_inc(max_rows_in, 16)

            def reshape_denominators(n):
                sp.wait_ge(den_out, n + 1)
                sp.dma_start(den_scratch, den[0:P:D, :]).then_inc(den_stored, 16)
                sp.wait_ge(den_stored, 16 * (n + 1))
                sp.dma_start(den_cols[:, :], den_scratch.rearrange("e (p j) -> (e p) j", j=2 * T // P)).then_inc(den_in, 16)
                sp.wait_ge(rec_small, n + 1)
                sp.dma_start(rec_scratch.rearrange("e (p j) -> (e p) j", j=2 * T // P), rec_cols[:, :]).then_inc(rec_stored, 16)
                if positive(n):
                    sp.wait_ge(o_done, n)
                sp.wait_ge(rec_stored, 16 * (n + 1))
                for e in range(2):
                    src = bass.AP(rec_scratch.tensor, e * T, [[0, D], [1, T]])
                    sp.dma_start(rec[own[e], :], src).then_inc(rec_in, 16)

            def store_o(n):
                sp.wait_ge(o_done, n + 1)
                sp.dma_start(o_pairs[n], o[:, :]).then_inc(o_stored, 16)

            load_qp(0)
            sp.wait_ge(memsets, MEMSETS)
            load_high(0, 0)
            store_offs(0, 0)
            load_qp(1)
            sp.wait_ge(consts_out, CONSTS_OUT)
            load_rel(0, 0)
            load_low(0, 0)
            load_v(0, 0)
            store_offs(1, 1)
            load_qp(2)
            for e in range(2):
                sp.wait_ge(rel_lo_done[e], 2)
            load_rel(1, 1)
            load_max_rows(0, 0)

            def pair(n, s):
                if before(n, NIT - 1):
                    if positive(SCORES * n):
                        sp.wait_ge(s_done, SCORES * n)
                    load_high(n + 1, 1 - s)
                if before(n, NIT - 2):
                    store_offs(n + 2, s)
                if before(n, NIT - 1):
                    load_low(n + 1, 1 - s)
                    if positive(KB * n):
                        sp.wait_ge(pv_done, KB * n)
                    load_v(n + 1, 1 - s)
                if positive(n):
                    reshape_denominators(n - 1)
                if positive(n - 1):
                    store_o(n - 2)
                if before(n, NIT - 2):
                    for e in range(2):
                        sp.wait_ge(rel_lo_done[e], 2 * (n + 2))
                if isinstance(n, int):
                    k = wp_part[n]
                    if k > 0:
                        sp.wait_ge(wp_lo_done, k)
                    sp.dma_start(wp_raw[:, :], proj_w_t[k * P:(k + 1) * P, :]).then_inc(wp_in, 16)
                if before(n, NIT - 3):
                    load_qp(n + 3)
                if before(n, NIT - 2):
                    load_rel(n + 2, s)
                if before(n, NIT - 1):
                    load_max_rows(n + 1, 1 - s)
            pairs(sp, pair)
            store_o(NIT - 2)
            reshape_denominators(NIT - 1)
            store_o(NIT - 1)
            sp.wait_ge(o_stored, 16 * NIT)

        @block.gpsimd
        def _(pool):
            def low_rows(n, s, axis):
                rel_low(pool, n, s, 1, axis)
                pool.wait_ge(rel_lo_done[1], 2 * n + axis + 1)

            nc.gpsimd.memset(offs[:, 0, 0:P], 0.0).then_inc(memsets, 1)
            nc.gpsimd.memset(ones[:, :], 1.0).then_inc(memsets, 1)
            for s in range(2):
                nc.gpsimd.memset(words(k_lo[s][:, :, :]), 0.0).then_inc(memsets, 1)
                nc.gpsimd.memset(words(q_max[s][:, :, :]), 0.0).then_inc(memsets, 1)
            nc.gpsimd.memset(mx[:, :], 0.0).then_inc(memsets, 1)
            pool.wait_ge(memsets, MEMSETS)
            low_rows(0, 0, 0)
            low_rows(0, 0, 1)

            def pair(n, s):
                for kb in range(1, KB):
                    if kb in (3, 4) and before(n, NIT - 1):
                        pool.wait_ge(sums[0], (KB - 1) * n + kb - 1)
                        low_rows(n + 1, 1 - s, kb - 3)
                    pool.wait_ge(exp_done, SCORES * n + 2 * kb + 1)
                    if kb == 1:
                        if positive(n):
                            pool.wait_ge(den_done, n)
                        nc.gpsimd.tensor_tensor(prob_sum[:, 0, :], prob[:, 0, 0, :], prob[:, 0, 1, :], ALU.add).then_inc(sums[0], 1)
                    else:
                        pool.wait_ge(sums[0], (KB - 1) * n + kb - 1)
                        nc.gpsimd.tensor_tensor(prob_sum[:, 0, :], prob_sum[:, 0, :], prob[:, 0, kb % SLOTS, :],
                                                ALU.add).then_inc(sums[0], 1)
            pairs(pool, pair)

        @block.scalar
        def _(act):
            act.wait_ge(consts_in, 16 * 7)
            nc.scalar.activation(table_hi[:, :], offs[:, 0, 0:P], ACT.Identity).then_inc(consts_out, 1)
            for s in range(2):
                for e in range(2):
                    nc.scalar.activation(k_hi[s][own[1 - e], e, :], rel[own[1 - e], :], ACT.Identity).then_inc(consts_out, 1)
            act.wait_ge(memsets, MEMSETS)
            for s in range(2):
                for e in range(2):
                    nc.scalar.activation(k_lo[s][max_row[e], e, :], rel[max_row[e], :], ACT.Identity,
                                         scale=0.0, bias=1.0).then_inc(consts_out, 1)
            act.wait_ge(tables_done, 1)

            def copy_offs(n, chunks=range(4)):
                for c in chunks:
                    e, half = c // 2, c % 2
                    act.wait_ge(offs_done, 4 * n + c + 1)
                    if half == 0 and positive(n):
                        act.wait_ge(offs_stored, 32 * n)
                    cols = slice(half * HALF, (half + 1) * HALF)
                    nc.scalar.activation(offs[own[0], e, cols], aux[own[0], cols], ACT.Identity).then_inc(offs_out, 1)
                    nc.scalar.activation(offs[own[1], e, :].rearrange("p (w h) -> p h w", h=HS)[:, half * HS // 2:(half + 1) * HS // 2, :],
                                         aux[own[1], cols].rearrange("p (h w) -> p h w", w=WS), ACT.Identity).then_inc(offs_out, 1)

            def rel_high(n, s):
                act.wait_ge(rel_in, 64 * (n + 1))
                for axis in range(2):
                    raw_rows, high, _ = rel_rows(n, s, 1, axis)
                    nc.scalar.activation(high, raw_rows, ACT.Identity).then_inc(rel_hi_done[1], 1)

            def copy_q(n, s):
                act.wait_ge(hi_in, 16 * 4 * (n + 1))
                for e in range(2):
                    nc.scalar.activation(q_max[s][own[e], e, :], words(q_hi[s][own[e], e, :]), ACT.Identity).then_inc(q_copied, 1)

            def copy_output(n):
                act.wait_ge(pv_done, KB * (n + 1))
                if positive(n):
                    act.wait_ge(o_done, n)
                nc.scalar.activation(raw[:, :], ps_o[:, :], ACT.Identity).then_inc(raw_out, 1)

            def copy_denominators(n):
                act.wait_ge(den_done, n + 1)
                if positive(n):
                    act.wait_ge(den_stored, 16 * n)
                nc.scalar.activation(den[:, :], aux[:, :], ACT.Identity).then_inc(den_out, 1)

            copy_offs(0)
            copy_offs(1)
            rel_high(0, 0)
            copy_q(0, 0)

            def exp(n, kb, e):
                act.wait_ge(s_done, SCORES * n + 2 * kb + e + 1)
                if positive(KB * n + kb - SLOTS + 1):
                    act.wait_ge(pv_done, KB * n + kb - SLOTS + 1)
                    summed = max(kb - SLOTS, 1) if kb >= SLOTS else kb - SLOTS + 1
                    act.wait_ge(sums[e], (KB - 1) * n + summed)
                nc.scalar.activation(prob[:, e, kb % SLOTS, :], ps_s[:, e, :], ACT.Exp).then_inc(exp_done, 1)

            def pair(n, s):
                if before(n, NIT - 2):
                    copy_offs(n + 2, (0, 1))
                for kb in range(KB):
                    for e in range(2):
                        exp(n, kb, e)
                        if kb == 1 and e == 0 and positive(n):
                            copy_denominators(n - 1)
                    if kb == 0 and before(n, NIT - 2):
                        copy_offs(n + 2, (2, 3))
                    if kb == 0 and positive(n):
                        copy_output(n - 1)
                    if kb == 2 and before(n, NIT - 1):
                        rel_high(n + 1, 1 - s)
                    if kb == 3 and before(n, NIT - 1):
                        copy_q(n + 1, 1 - s)
                    if kb == 5 and isinstance(n, int):
                        k = wp_part[n]
                        act.wait_ge(wp_in, 16 * (k + 1))
                        nc.scalar.activation(wp_hi[:, k, :], wp_raw[:, :], ACT.Identity).then_inc(wp_hi_done, 1)
            pairs(act, pair)
            copy_output(NIT - 1)
            copy_denominators(NIT - 1)

        @block.vector
        def _(dve):
            dve.wait_ge(consts_out, 1)
            nc.vector.tensor_tensor(table_lo[:, :], offs[:, 0, 0:P], words(table_hi[:, :]), ALU.subtract).then_inc(tables_done, 1)
            dve.wait_ge(memsets, MEMSETS)

            def split_rel(n, s):
                dve.wait_ge(rel_in, 64 * (n + 1))
                if positive(SCORES * (n - 1)):
                    dve.wait_ge(s_done, SCORES * (n - 1))
                for axis in range(2):
                    raw_rows, high, _ = rel_rows(n, s, 0, axis)
                    nc.vector.tensor_copy(high, raw_rows).then_inc(rel_hi_done[0], 1)
                for axis in range(2):
                    rel_low(dve, n, s, 0, axis)

            def row_max(n, t):
                dve.wait_ge(tile_done, TILES * n + t + 1)
                if t == 0 and positive(n):
                    dve.wait_ge(max_ready, n)
                nc.vector.reduce_max(half_max[:, t:t + 1], aux[:, (t % 2) * HALF:(t % 2 + 1) * HALF], AX_X).then_inc(max_done, 1)

            def negate_max(n):
                dve.wait_ge(max_done, TILES * (n + 1))
                if positive(n):
                    dve.wait_ge(max_t_ps, n)
                nc.vector.reduce_max(mx[:, 0:2 * KB], half_max[:, :].rearrange("p (t h) -> p t h", h=2), AX_X).then_inc(max_ready, 1)
                dve.wait_ge(max_t_ps, n + 1)
                if positive(n):
                    dve.wait_ge(max_rows_in, 32 * n)
                nc.vector.tensor_scalar(mx_t[:, :], aux[0:2 * KB, 0:P], -1.0, None, ALU.mult).then_inc(max_t_done, 1)

            def add(n, kb):
                dve.wait_ge(exp_done, SCORES * n + 2 * kb + 2)
                if kb == 1:
                    if positive(n):
                        dve.wait_ge(den_done, n)
                    nc.vector.tensor_tensor(prob_sum[:, 1, :], prob[:, 1, 0, :], prob[:, 1, 1, :], ALU.add).then_inc(sums[1], 1)
                else:
                    dve.wait_ge(sums[1], (KB - 1) * n + kb - 1)
                    nc.vector.tensor_tensor(prob_sum[:, 1, :], prob_sum[:, 1, :], prob[:, 1, kb % SLOTS, :],
                                            ALU.add).then_inc(sums[1], 1)

            def invert_denominators(n):
                dve.wait_ge(den_in, 16 * (n + 1))
                if positive(n):
                    dve.wait_ge(rec_stored, 16 * n)
                nc.vector.reciprocal(rec_cols[:, :], den_cols[:, :]).then_inc(rec_small, 1)

            def normalise(n):
                dve.wait_ge(rec_in, 32 * (n + 1))
                dve.wait_ge(raw_out, n + 1)
                if positive(n):
                    dve.wait_ge(o_stored, 16 * n)
                nc.vector.tensor_tensor(o[:, :], raw[:, :], rec[:, :], ALU.mult).then_inc(o_done, 1)

            split_rel(0, 0)
            for t in range(TILES):
                row_max(0, t)
            negate_max(0)

            def pair(n, s):
                if positive(n):
                    add(n - 1, KB - 1)
                if positive(n - 1):
                    normalise(n - 2)
                if before(n, NIT - 1):
                    split_rel(n + 1, 1 - s)
                for kb in range(1, KB):
                    tiles = range(FIRST_TILE[kb], FIRST_TILE[kb] + PER_STEP[kb]) if before(n, NIT - 1) else ()
                    for t in tiles[:-1]:
                        row_max(n + 1, t)
                    if kb >= 2:
                        add(n, kb - 1)
                    for t in tiles[-1:]:
                        row_max(n + 1, t)
                    if kb == 4 and positive(n):
                        invert_denominators(n - 1)
                    if kb == 6 and isinstance(n, int):
                        k = wp_part[n]
                        dve.wait_ge(wp_hi_done, k + 1)
                        nc.vector.tensor_tensor(wp_lo[:, k, :], wp_raw[:, :], words(wp_hi[:, k, :]),
                                                ALU.subtract).then_inc(wp_lo_done, 1)
                if before(n, NIT - 1):
                    negate_max(n + 1)
            pairs(dve, pair)
            add(NIT - 1, KB - 1)
            normalise(NIT - 2)
            invert_denominators(NIT - 1)
            normalise(NIT - 1)

        @block.tensor
        def _(pe):
            def offsets(n, chunks=range(4)):
                pe.wait_ge(qp_in, 32 * (n + 1))
                for c in chunks:
                    e, half = c // 2, c % 2
                    cols = slice(half * HALF, (half + 1) * HALF)
                    if c < 2:
                        if positive(n - 1):
                            pe.wait_ge(max_t_done, n - 1)
                        elif isinstance(n, int) and n == 1:
                            pe.wait_ge(offs_out, 8)
                    else:
                        pe.wait_ge(offs_out, 8 * n + 2 * (c - 1))
                    nc.tensor.matmul(aux[:, cols], table_hi[:, :], qp[:, e, cols], start=True, stop=False)
                    nc.tensor.matmul(aux[:, cols], table_lo[:, :], qp[:, e, cols], start=False, stop=True).then_inc(offs_done, 1)

            def max_tile(n, s, t):
                e, qb, half = t // (2 * KB), t // 2 % KB, t % 2
                if t == 0:
                    if before(n, NIT - 1):
                        pe.wait_ge(offs_out, 8 * (n + 2))
                    if positive(n - 1):
                        pe.wait_ge(den_out, n - 1)
                    pe.wait_ge(hi_in, 16 * 4 * (n + 1))
                if t >= 2:
                    pe.wait_ge(max_done, TILES * n + t - 1)
                if t % (2 * KB) == 0:
                    pe.wait_ge(rel_hi_done[e], 2 * (n + 1))
                mm = nc.tensor.matmul(aux[:, half * HALF:(half + 1) * HALF], q_hi[s][:, e, qb * P:(qb + 1) * P],
                                      k_hi[s][:, e, half * HALF:(half + 1) * HALF], start=True, stop=True)
                mm.then_inc(tile_done, 1)

            def transpose_max(n):
                pe.wait_ge(max_ready, n + 1)
                nc.tensor.transpose(aux[:, 0:P], mx[:, :], ident[:, :]).then_inc(max_t_ps, 1)

            def scores(n, s, e, kb, j):
                keys = slice(kb * P, (kb + 1) * P)
                if j == 0:
                    if kb == 0 and e == 0:
                        pe.wait_ge(lo_v_in, 16 * 5 * (n + 1))
                        for i in range(2):
                            pe.wait_ge(rel_lo_done[i], 2 * (n + 1))
                        pe.wait_ge(q_copied, 2 * (n + 1))
                    if positive(SCORES * n + 2 * (kb - 1) + e + 1):
                        pe.wait_ge(exp_done, SCORES * n + 2 * (kb - 1) + e + 1)
                if j == 2 and kb == 0 and e == 0:
                    pe.wait_ge(max_rows_in, 32 * (n + 1))
                k, q = ((k_hi, q_hi), (k_hi, q_lo), (k_lo, q_max))[j]
                for half in range(2):
                    cols = slice(half * HALF, (half + 1) * HALF)
                    mm = nc.tensor.matmul(ps_s[:, e, cols], k[s][:, e, keys], q[s][:, e, cols],
                                          start=(j == 0), stop=(j == 2))
                if j == 2:
                    mm.then_inc(s_done, 1)

            def values(n, s, kb):
                pe.wait_ge(exp_done, SCORES * n + 2 * kb + 2)
                for half in range(2):
                    for e in range(2):
                        cols = slice(half * HALF, (half + 1) * HALF)
                        mm = nc.tensor.matmul(ps_o[own[e], cols], v[s][:, kb, own[e]], prob[:, e, kb % SLOTS, cols],
                                              start=(kb == 0), stop=(kb == KB - 1))
                mm.then_inc(pv_done, 1)

            def denominators(n):
                if before(n, NIT - 3):
                    pe.wait_ge(offs_out, 8 * (n + 4))
                if before(n, NIT - 1):
                    pe.wait_ge(max_t_done, n + 2)
                for e in range(2):
                    pe.wait_ge(sums[e], (KB - 1) * (n + 1))
                for half in range(2):
                    for e in range(2):
                        cols = slice(half * HALF, (half + 1) * HALF)
                        mm = nc.tensor.matmul(aux[own[e], cols], ones[:, :], prob_sum[:, e, cols], start=True, stop=True)
                mm.then_inc(den_done, 1)

            pe.wait_ge(memsets, MEMSETS)
            pe.wait_ge(consts_out, CONSTS_OUT)
            pe.wait_ge(tables_done, 1)
            offsets(0)
            offsets(1)
            for t in range(TILES):
                max_tile(0, 0, t)
            transpose_max(0)

            def first_step(n, s):
                more = before(n, NIT - 2)
                for e in range(2):
                    scores(n, s, e, 0, 0)
                    if e == 1 and positive(n):
                        transpose_max(n)
                    scores(n, s, e, 0, 1)
                if more:
                    offsets(n + 2, (0, 1))
                if positive(n):
                    values(n - 1, 1 - s, KB - 1)
                for e in range(2):
                    scores(n, s, e, 0, 2)
                    if more:
                        offsets(n + 2, (2 + e,))

            def step(n, s, kb):
                t, last = FIRST_TILE[kb], FIRST_TILE[kb] + PER_STEP[kb] if before(n, NIT - 1) else 0
                before_score = (0, 2, 3, 5) if PER_STEP[kb] == 6 else (0, 2, 4)

                def tile():
                    nonlocal t
                    if t < last:
                        max_tile(n + 1, 1 - s, t)
                        t += 1
                for i in range(6):
                    if i in before_score and kb > 1:
                        tile()
                    scores(n, s, i // 3, kb, i % 3)
                if kb > 1:
                    tile()
                elif positive(n):
                    denominators(n - 1)
                    pe.wait_ge(raw_out, n)
                values(n, s, kb - 1)
                tile()

            def pair(n, s):
                first_step(n, s)
                for kb in range(1, KB):
                    step(n, s, kb)
            pairs(pe, pair)
            values(NIT - 1, 1, KB - 1)
            denominators(NIT - 1)


def project_out(nc, x_t, o_pairs, w_hi, w_lo, v_bias_cols, bias_cols, out_t):
    with ExitStack() as ctx:
        sb = lambda name, shape, dt: ctx.enter_context(nc.sbuf_tensor(name, shape, dt))
        sem = lambda name: ctx.enter_context(nc.semaphore(name))
        o_raw = sb("o_raw", [P, 2, CB, HALF], F32)
        o_hi = sb("o_hi", [P, 2, CB, HALF], F32R)
        o_lo = sb("o_lo", [P, 2, CB, HALF], F32R)
        x_res = sb("x_res", [P, 2, CB, HALF], F32)
        y = sb("y", [P, CB, HALF], F32)
        v_bias = sb("o_bias", [P, CB], F32)
        bias = sb("p_bias", [P, CB], F32)
        ps = ctx.enter_context(nc.psum_tensor("ps_y", [P, CB, HALF], F32))
        bias_in = sem("p3_bias_in")
        o_in = [sem(f"o_in{i}") for i in range(2)]
        x_in = [sem(f"res_in{i}") for i in range(2)]
        o_hi_done, o_lo_done = sem("o_hi_done"), sem("o_lo_done")
        block_done, y_done = sem("block_done"), sem("y_done")
        y_stored = [sem(f"y_stored{i}") for i in range(CB)]
        block = ctx.enter_context(nc.Block())

        @block.sync
        def _(sp):
            sp.dma_start(v_bias[:, :], v_bias_cols).then_inc(bias_in, 16)
            sp.dma_start(bias[:, :], bias_cols).then_inc(bias_in, 16)

            def load_o(i, h):
                cols = slice(h * HALF, (h + 1) * HALF)
                sp.dma_start(o_raw[:, h], o_pairs[i].rearrange("j p t -> p j t")[:, :, cols]).then_inc(o_in[h], 16)

            def load_x(i, h):
                cols = slice(h * HALF, (h + 1) * HALF)
                sp.dma_start(x_res[:, h], x_t[i].rearrange("(k p) t -> p k t", p=P)[:, :, cols]).then_inc(x_in[h], 16)

            for load in (load_o, load_x):
                for h in range(2):
                    load(0, h)

            def image(i, last):
                for h in range(2):
                    n = 2 * i + h
                    for g in range(CB):
                        sp.wait_ge(y_done, n * CB + g + 1)
                        sp.dma_start(out_t[i, g * P:(g + 1) * P, h * HALF:(h + 1) * HALF], y[:, g, :]).then_inc(y_stored[g], 16)
                    if not last:
                        sp.wait_ge(o_lo_done, n + 1)
                        load_o(i + 1, h)
                        load_x(i + 1, h)
            image(0, False)
            with sp.Fori(1, B - 1) as i:
                image(i, False)
            image(B - 1, True)
            for g in range(CB):
                sp.wait_ge(y_stored[g], 16 * 2 * B)

        @block.scalar
        def _(act):
            act.wait_ge(bias_in, 32)

            def split_hi(i, h, n):
                act.wait_ge(o_in[h], 16 * (i + 1))
                if not (isinstance(n, int) and n < 2):
                    act.wait_ge(block_done, (n - 1) * CB)
                for k in range(CB):
                    nc.scalar.activation(o_hi[:, h, k, :], o_raw[:, h, k, :], ACT.Identity,
                                         bias=v_bias[:, k:k + 1]).then_inc(o_hi_done, 1)
            split_hi(0, 0, 0)
            split_hi(0, 1, 1)
            with act.Fori(0, B - 1) as i:
                for h in range(2):
                    split_hi(i + 1, h, 2 * i + 2 + h)

        @block.vector
        def _(dve):
            dve.wait_ge(bias_in, 32)

            def split_lo(n, h):
                for k in range(CB):
                    dve.wait_ge(o_hi_done, n * CB + k + 1)
                    op = nc.vector.scalar_tensor_tensor(o_lo[:, h, k, :], o_raw[:, h, k, :], v_bias[:, k:k + 1],
                                                        words(o_hi[:, h, k, :]), ALU.add, ALU.subtract)
                op.then_inc(o_lo_done, 1)

            def finish(i, n, h):
                for g in range(CB):
                    dve.wait_ge(block_done, n * CB + g + 1)
                    if g == 0:
                        dve.wait_ge(x_in[h], 16 * (i + 1))
                    if positive(16 * n):
                        dve.wait_ge(y_stored[g], 16 * n)
                    nc.vector.scalar_tensor_tensor(y[:, g, :], ps[:, g, :], bias[:, g:g + 1], x_res[:, h, g, :],
                                                   ALU.add, ALU.add).then_inc(y_done, 1)
            split_lo(0, 0)
            split_lo(1, 1)

            def image(i):
                for h in range(2):
                    finish(i, 2 * i + h, h)
                    split_lo(2 * i + h + 2, h)
            image(0)
            with dve.Fori(1, B - 1) as i:
                image(i)
            for h in range(2):
                finish(B - 1, 2 * (B - 1) + h, h)

        @block.tensor
        def _(pe):
            def image(i, first):
                for h in range(2):
                    n = 2 * i + h
                    pe.wait_ge(o_lo_done, n + 1)
                    for g in range(CB):
                        if not (first and h == 0):
                            pe.wait_ge(y_done, (n - 1) * CB + g + 1)
                        cols = slice(g * P, (g + 1) * P)
                        for k in range(CB):
                            for j, (w, o) in enumerate(((w_hi, o_hi), (w_hi, o_lo), (w_lo, o_hi))):
                                mm = nc.tensor.matmul(ps[:, g, :], w[:, k, cols], o[:, h, k, :],
                                                      start=(k == 0 and j == 0), stop=(k == CB - 1 and j == 2))
                        mm.then_inc(block_done, 1)
            image(0, True)
            with pe.Fori(1, B) as i:
                image(i, False)


def build(nc, io):
    scratch = lambda name, shape: nc.dram_tensor(name, shape, F32, kind="Internal").ap()
    qk_hi = [scratch(f"{n}_hi_d", (NIT, P, T)) for n in "qk"]
    qk_lo = [scratch(f"{n}_lo_d", (NIT, P, T)) for n in "qk"]
    v_d = scratch("v_d", (NIT, P, KB, P))
    rel_scratch = scratch("rel_d", (2, 2, P, T))
    den_scratch, rec_scratch = scratch("den_d", (2, T)), scratch("rec_d", (2, T))
    o_d = scratch("o_d", (NIT, P, T))
    by_image = lambda ap: ap.rearrange("(i j) p t -> i (j p) t", j=NPAIR)
    project_qkv(nc, io["x_t"], io["qkv_w_t"], io["qk_bias"], io["group_mean"],
                [by_image(a) for a in qk_hi], [by_image(a) for a in qk_lo],
                v_d.rearrange("(i j) p k d -> i j p k d", j=NPAIR))
    with ExitStack() as ctx:
        wp_hi, wp_lo = (ctx.enter_context(nc.sbuf_tensor(name, [P, CB, C], F32R)) for name in ("wp_hi", "wp_lo"))
        attend(nc, qk_hi, qk_lo, v_d, (io["rel_h_t"], io["rel_w_t"]), io["one_hots"], io["identity"], rel_scratch,
               den_scratch, rec_scratch, o_d, io["proj_w_t"], wp_hi, wp_lo)
        project_out(nc, io["x_t"], o_d.rearrange("(i j) p t -> i j p t", j=NPAIR), wp_hi, wp_lo, io["v_bias"],
                    io["proj_bias"], io["out_t"])


def shape_constants():
    q = np.arange(P) // PER_GROUP
    token = np.arange(T)
    j = np.arange(HS)[:, None]
    return {
        "group_mean": (q[:, None] == q[None, :]).astype(np.float32) / PER_GROUP,
        "one_hots": np.concatenate([HS - 1 - j == token // WS, WS - 1 - j == token % WS]).astype(np.float32),
        "identity": np.eye(P, dtype=np.float32),
    }


def kernel(x, L0_conv_qkv_w, L0_conv_qkv_b, L0_conv_proj_w, L0_conv_proj_b, L0_conv_rel_pos_h, L0_conv_rel_pos_w):
    import concourse.bacc as bacc
    from concourse.bass_utils import run_bass_kernel_spmd

    cols = lambda v: np.ascontiguousarray(np.asarray(v).reshape(-1, P).T)
    qkv_b = np.asarray(L0_conv_qkv_b)
    arrays = {
        "x_t": np.ascontiguousarray(np.asarray(x).reshape(B, T, C).transpose(0, 2, 1)),
        "qkv_w_t": np.ascontiguousarray(np.asarray(L0_conv_qkv_w).T),
        "proj_w_t": np.ascontiguousarray(np.asarray(L0_conv_proj_w).T),
        "qk_bias": cols(qkv_b[:2 * C]),
        "v_bias": cols(qkv_b[2 * C:]),
        "proj_bias": cols(L0_conv_proj_b),
        "rel_h_t": np.ascontiguousarray(np.asarray(L0_conv_rel_pos_h).T),
        "rel_w_t": np.ascontiguousarray(np.asarray(L0_conv_rel_pos_w).T),
        **shape_constants(),
    }
    nc = bacc.Bacc("TRN2", target_bir_lowering=False, num_devices=1)
    io = {n: nc.dram_tensor(n, a.shape, F32, kind="ExternalInput").ap() for n, a in arrays.items()}
    io["out_t"] = nc.dram_tensor("out_t", (B, C, T), F32, kind="ExternalOutput").ap()
    build(nc, io)
    result = run_bass_kernel_spmd(nc, [arrays], core_ids=[0])
    out = result.results[0]["out_t"]
    return np.ascontiguousarray(out.transpose(0, 2, 1)).reshape(B, HS, WS, C)
```

```python
from contextlib import ExitStack

import numpy as np
import concourse.bass as bass
from concourse import mybir

F32 = mybir.dt.float32
F32R = mybir.dt.float32r
ACT = mybir.ActivationFunctionType
ALU = mybir.AluOpType
AX_X = mybir.AxisListType.X

P = 128
B, HS, WS, C = 8, 32, 32, 768
T = HS * WS
HALF = T // 2
NH, D = 12, 64
NPAIR = NH // 2
NIT = B * NPAIR
CB = C // P
KB = T // P
NREL = 2 * HS - 1
GROUP = C // 32
PER_GROUP = GROUP // CB
EPS = 1e-5
SCALE = float(D) ** -0.5


def positive(value):
    return not isinstance(value, int) or value > 0


def words(ap):
    return ap.bitcast(F32)


def project_qkv(nc, x_t, w_t, bias_cols, group_mean, qk_hi, qk_lo, v_rows):
    QK = 2 * CB
    VN = C // 2
    VG = 2 * (HALF // P)
    NG = QK + VG
    BANKS, SLOTS = 5, 4
    with ExitStack() as ctx:
        sb = lambda name, shape, dt: ctx.enter_context(nc.sbuf_tensor(name, shape, dt))
        sem = lambda name: ctx.enter_context(nc.semaphore(name))
        w_hi = sb("w_hi", [P, CB, 3 * C], F32R)
        w_lo = sb("w_lo", [P, CB, 3 * C], F32R)
        x_hi = sb("x_hi", [P, 2, CB, HALF], F32R)
        x_lo = sb("x_lo", [P, 2, CB, HALF], F32R)
        x_raw = sb("x_raw", [P, CB, T], F32)
        out_slots = sb("out_slots", [P, SLOTS * (2 * HALF + VN)], F32)
        out_hi, out_lo = (out_slots[:, i * SLOTS * HALF:(i + 1) * SLOTS * HALF].rearrange("p (s t) -> p s t", s=SLOTS) for i in range(2))
        out_v = out_slots[:, 2 * SLOTS * HALF:].rearrange("p (s t) -> p s t", s=SLOTS)
        q_stages = [out_slots[:, at:at + 2 * C].rearrange("p (k n) -> p k n", k=2)
                    for at in (0, 2 * C, SLOTS * (2 * HALF + VN) - 2 * C)]
        kv_stages = [q_stages[2][:, i, :] for i in range(2)]
        bias = sb("bias", [P, QK], F32)
        averager = sb("averager", [P, P], F32)
        stats = sb("stats", [P, 2 * CB, 6], F32)
        moments = sb("moments", [P, 2], F32)
        gmean = sb("gmean", [P, 2], F32)
        shift = sb("shift", [P, 2], F32)
        spread = sb("spread", [P, 2], F32)
        gvar = sb("gvar", [P, 2], F32)
        std = sb("std", [P, 2], F32)
        rstd = sb("rstd", [P, 2], F32)
        ps = ctx.enter_context(nc.psum_tensor("ps_qkv", [P, BANKS, HALF], F32))
        ps_stat = ctx.enter_context(nc.psum_tensor("ps_stat", [P, HALF], F32))

        consts_in = sem("p1_consts_in")
        wq_in = [sem(f"wq_in{i}") for i in range(3)]
        wkv_in = [sem(f"wkv_in{i}") for i in range(2)]
        w_hi_done = sem("w_hi_done")
        q_lo_done, kv_lo_done = sem("q_lo_done"), sem("kv_lo_done")
        x0_in = [sem(f"x0_in{i}") for i in range(2)]
        x_in = sem("x_in")
        dve_step = sem("dve_step")
        part_mean, gmean_ps, part_var, gvar_ps = sem("part_mean"), sem("gmean_ps"), sem("part_var"), sem("gvar_ps")
        var_ready, std_ready = sem("var_ready"), sem("std_ready")
        x_normed, x_hi_done, x_lo_done = sem("x_normed"), sem("x_hi_done"), sem("x_lo_done")
        group_done = sem("group_done")
        hi_out, lo_out = sem("hi_out"), sem("lo_out")
        v_out = sem("v_out")
        qk_stored = [sem(f"qk_stored{i}") for i in range(SLOTS)]
        v_stored = [sem(f"v_stored{i}") for i in range(SLOTS)]
        block = ctx.enter_context(nc.Block())

        def q_part(tensor, c):
            return tensor[:, 2 * c:2 * c + 2, 0:C]

        def kv_part(tensor, c):
            n = 1 + c // CB
            return tensor[:, c % CB, n * C:(n + 1) * C]

        kv_scale = lambda c: SCALE if c < CB else 1.0

        @block.sync
        def _(sp):
            sp.dma_start(bias[:, :], bias_cols).then_inc(consts_in, 16)
            sp.dma_start(averager[:, :], group_mean).then_inc(consts_in, 16)
            x0 = x_t[0].rearrange("(p k) t -> p k t", k=CB)
            for c in range(2):
                ks = slice(c * CB // 2, (c + 1) * CB // 2)
                sp.dma_start(x_raw[:, ks, :], x0[:, ks, :]).then_inc(x0_in[c], 16)
            w_rows = w_t.rearrange("(p k) n -> p k n", k=CB)

            def load_kv(c):
                if c >= 2:
                    sp.wait_ge(kv_lo_done, c - 1)
                sp.dma_start(kv_stages[c % 2], kv_part(w_rows, c)).then_inc(wkv_in[c % 2], 16)

            for c in range(3):
                sp.dma_start(q_stages[c], q_part(w_rows, c)).then_inc(wq_in[c], 16)
            sp.wait_ge(q_lo_done, 3)
            load_kv(0)
            load_kv(1)

            def image(i, last):
                for h in range(2):
                    n = 2 * i + h
                    for g in range(QK):
                        sp.wait_ge(lo_out, n * QK + g + 1)
                        rows = slice((g % CB) * P, (g % CB + 1) * P)
                        cols = slice(h * HALF, (h + 1) * HALF)
                        s = g % SLOTS
                        sp.dma_start(qk_hi[g // CB][i, rows, cols], out_hi[:, s, :]).then_inc(qk_stored[s], 16)
                        sp.dma_start(qk_lo[g // CB][i, rows, cols], out_lo[:, s, :]).then_inc(qk_stored[s], 16)
                        first = isinstance(n, int) and n == 0
                        if first and g + 2 < 2 * CB:
                            load_kv(g + 2)
                        if h == 0 and g == (9 if first else 1) and not last:
                            sp.wait_ge(x_lo_done, 2 * i + 2)
                            sp.dma_start(x_raw[:, :, :], x_t[i + 1].rearrange("(p k) t -> p k t", k=CB)).then_inc(x_in, 16)
                    for g in range(VG):
                        sp.wait_ge(v_out, VG + n * VG + g + 1)
                        kb, c = h * (HALF // P) + g // 2, g % 2
                        dst = v_rows[i, c * (NPAIR // 2):(c + 1) * (NPAIR // 2), :, kb, :].rearrange("j p d -> p j d")
                        sp.dma_start(dst, out_v[:, g % SLOTS, :].rearrange("p (j d) -> p j d", d=P)).then_inc(v_stored[g % SLOTS], 16)
            image(0, False)
            with sp.Fori(1, B - 1) as i:
                image(i, False)
            image(B - 1, True)
            for s in range(SLOTS):
                sp.wait_ge(qk_stored[s], 32 * 2 * B * QK // SLOTS)
                sp.wait_ge(v_stored[s], 16 * 2 * B * VG // SLOTS)

        @block.scalar
        def _(act):
            act.sem_inc(v_out, VG)

            def split_kv_hi(c):
                act.wait_ge(wkv_in[c % 2], 16 * (c // 2 + 1))
                nc.scalar.activation(kv_part(w_hi, c), kv_stages[c % 2], ACT.Identity, scale=kv_scale(c)).then_inc(w_hi_done, 1)

            def deviation(i):
                act.wait_ge(var_ready, i + 1)
                nc.scalar.activation(std[:, :], gvar[:, :], ACT.Sqrt).then_inc(std_ready, 1)

            def split_hi(n, h):
                act.wait_ge(x_normed, n + 1)
                nc.scalar.activation(x_hi[:, h], x_raw[:, :, h * HALF:(h + 1) * HALF], ACT.Identity).then_inc(x_hi_done, 1)

            def image(i, last):
                split_hi(2 * i + 1, 1)
                for h in range(2):
                    n = 2 * i + h
                    if h == 1 and not last:
                        split_hi(2 * i + 2, 0)
                    for g in range(QK):
                        if isinstance(n, int) and n == 0:
                            split_kv_hi(g)
                        s = g % SLOTS
                        if positive(32 * (n * (QK // SLOTS) + g // SLOTS)):
                            act.wait_ge(qk_stored[s], 32 * (n * (QK // SLOTS) + g // SLOTS))
                        act.wait_ge(group_done, n * NG + g + 1)
                        nc.scalar.activation(out_hi[:, s, :].bitcast(F32R), ps[:, g % BANKS, :], ACT.Identity,
                                             bias=bias[:, g:g + 1]).then_inc(hi_out, 1)
                    for g in range(VG):
                        if g == (7 if isinstance(n, int) and n == 0 else 5) and h == 0 and not last:
                            deviation(i + 1)
                        if positive(16 * (n * (VG // SLOTS) + g // SLOTS)):
                            act.wait_ge(v_stored[g % SLOTS], 16 * (n * (VG // SLOTS) + g // SLOTS))
                        act.wait_ge(group_done, n * NG + QK + g + 1)
                        nc.scalar.activation(out_v[:, g % SLOTS, :], ps[:, (QK + g) % BANKS, 0:VN],
                                             ACT.Identity).then_inc(v_out, 1)
            for c in range(3):
                if c == 2:
                    deviation(0)
                act.wait_ge(wq_in[c], 16)
                nc.scalar.activation(q_part(w_hi, c), q_stages[c], ACT.Identity).then_inc(w_hi_done, 1)
            split_hi(0, 0)
            image(0, False)
            with act.Fori(1, B - 1) as i:
                image(i, False)
            image(B - 1, True)

        @block.gpsimd
        def _(pool):
            for c in range(3):
                pool.wait_ge(w_hi_done, c + 1)
                nc.gpsimd.tensor_tensor(q_part(w_lo, c), q_stages[c], words(q_part(w_hi, c)), ALU.subtract).then_inc(q_lo_done, 1)

        @block.vector
        def _(dve):
            dve.wait_ge(consts_in, 32)
            nc.vector.tensor_scalar(bias[:, CB:QK], bias[:, CB:QK], SCALE, None, ALU.mult).then_inc(dve_step, 1)

            def split_kv_lo(c):
                dve.wait_ge(w_hi_done, 3 + c + 1)
                nc.vector.scalar_tensor_tensor(kv_part(w_lo, c), kv_stages[c % 2], kv_scale(c), words(kv_part(w_hi, c)),
                                               ALU.mult, ALU.subtract).then_inc(kv_lo_done, 1)

            STEPS = 2 * CB + 6

            def statistics(i):
                base = 1 + i * STEPS
                first = isinstance(i, int) and i == 0
                if not first:
                    dve.wait_ge(x_in, 16 * i)
                for j in range(2 * CB):
                    if first and j % CB == 0:
                        dve.wait_ge(x0_in[j // CB], 16)
                    nc.vector.bn_stats(stats[:, j, :], x_raw[:, j // 2, (j % 2) * HALF:(j % 2 + 1) * HALF]).then_inc(dve_step, 1)
                dve.wait_ge(dve_step, base + 2 * CB)
                nc.vector.memset(spread[:, :], 0.0)
                nc.vector.bn_aggr(moments[:, :], stats[:, :, :].rearrange("p a b -> p (a b)")).then_inc(part_mean, 1)

            def group_variance(i):
                base = 1 + i * STEPS + 2 * CB
                dve.wait_ge(gmean_ps, i + 1)
                nc.vector.tensor_copy(gmean[:, :], ps_stat[:, 0:2]).then_inc(dve_step, 1)
                dve.wait_ge(dve_step, base + 1)
                nc.vector.tensor_tensor(shift[:, :], moments[:, :], gmean[:, :], ALU.subtract).then_inc(dve_step, 1)
                dve.wait_ge(dve_step, base + 2)
                nc.vector.tensor_tensor(spread[:, :], shift[:, :], shift[:, :], ALU.mult).then_inc(dve_step, 1)
                dve.wait_ge(dve_step, base + 3)
                nc.vector.tensor_tensor(spread[:, 1:2], spread[:, 0:1], moments[:, 1:2], ALU.add).then_inc(part_var, 1)

            def reciprocal_deviation(i):
                base = 1 + i * STEPS + 2 * CB + 3
                dve.wait_ge(gvar_ps, i + 1)
                nc.vector.tensor_scalar(gvar[:, :], ps_stat[:, 0:2], EPS, None, ALU.add).then_inc(var_ready, 1)
                dve.wait_ge(std_ready, i + 1)
                nc.vector.reciprocal(rstd[:, :], std[:, :]).then_inc(dve_step, 3)

            def normalise(n, h, i):
                dve.wait_ge(dve_step, 1 + (i + 1) * STEPS)
                if positive((n - 1) * NG):
                    dve.wait_ge(group_done, (n - 1) * NG)
                xh = x_raw[:, :, h * HALF:(h + 1) * HALF]
                nc.vector.tensor_scalar(xh, xh, gmean[:, 0:1], rstd[:, 1:2], ALU.subtract, ALU.mult).then_inc(x_normed, 1)
                dve.wait_ge(x_hi_done, n + 1)
                nc.vector.tensor_tensor(x_lo[:, h], xh, words(x_hi[:, h]), ALU.subtract).then_inc(x_lo_done, 1)

            def image(i, last):
                normalise(2 * i + 1, 1, i)
                for h in range(2):
                    n = 2 * i + h
                    if h == 1 and not last:
                        normalise(2 * i + 2, 0, i + 1)
                    for g in range(QK):
                        s = g % SLOTS
                        first = isinstance(n, int) and n == 0
                        if first:
                            split_kv_lo(g)
                        if h == 0 and g == 6 and not first and not last:
                            statistics(i + 1)
                        if h == 0 and g == 11 and not first and not last:
                            group_variance(i + 1)
                        dve.wait_ge(hi_out, n * QK + g + 1)
                        nc.vector.scalar_tensor_tensor(out_lo[:, s, :].bitcast(F32R), ps[:, g % BANKS, :], bias[:, g:g + 1],
                                                       out_hi[:, s, :], ALU.add, ALU.subtract).then_inc(lo_out, 1)
                    if isinstance(n, int) and n == 0:
                        statistics(1)
                        group_variance(1)
                    if h == 0 and not last:
                        reciprocal_deviation(i + 1)
            statistics(0)
            group_variance(0)
            reciprocal_deviation(0)
            normalise(0, 0, 0)
            image(0, False)
            with dve.Fori(1, B - 1) as i:
                image(i, False)
            image(B - 1, True)

        @block.tensor
        def _(pe):
            def group_average(done, ready, col, i):
                pe.wait_ge(ready, i + 1)
                nc.tensor.matmul(ps_stat[:, 0:2], averager[:, :], col, start=True, stop=True).then_inc(done, 1)

            def image(i, last):
                for h in range(2):
                    n = 2 * i + h
                    pe.wait_ge(x_lo_done, n + 1)
                    for g in range(NG):
                        if isinstance(n, int) and n == 0 and g in (QK // 2, QK):
                            pe.wait_ge(kv_lo_done, CB if g < QK else 2 * CB)
                        if BANKS <= g < BANKS + QK:
                            pe.wait_ge(lo_out, n * QK + g - BANKS + 1)
                        else:
                            before = g - BANKS - QK if g >= BANKS else g - BANKS
                            pe.wait_ge(v_out, VG + n * VG + before + 1)
                        if g < QK:
                            out = ps[:, g % BANKS, :]
                            cols = slice(g * P, (g + 1) * P)
                            for k in range(CB):
                                a = [(w_hi, x_hi), (w_hi, x_lo), (w_lo, x_hi)]
                                for j, (w, x) in enumerate(a):
                                    last_mm = nc.tensor.matmul(out, w[:, k, cols], x[:, h, k, :],
                                                               start=(k == 0 and j == 0), stop=(k == CB - 1 and j == 2))
                        else:
                            t, c = (g - QK) // 2, (g - QK) % 2
                            out = ps[:, g % BANKS, 0:VN]
                            toks = slice(t * P, (t + 1) * P)
                            cols = slice(2 * C + c * VN, 2 * C + (c + 1) * VN)
                            for k in range(CB):
                                a = [(x_hi, w_hi), (x_hi, w_lo), (x_lo, w_hi)]
                                for j, (x, w) in enumerate(a):
                                    last_mm = nc.tensor.matmul(out, x[:, h, k, toks], w[:, k, cols],
                                                               start=(k == 0 and j == 0), stop=(k == CB - 1 and j == 2))
                        last_mm.then_inc(group_done, 1)
                        first = isinstance(n, int) and n == 0
                        if h == 0 and not last and g == (QK + 5 if first else QK - 2):
                            group_average(gmean_ps, part_mean, moments[:, :], i + 1)
                        if h == 0 and not last and g == (QK + 7 if first else QK + 2):
                            group_average(gvar_ps, part_var, spread[:, 0:2], i + 1)
            pe.wait_ge(consts_in, 32)
            group_average(gmean_ps, part_mean, moments[:, :], 0)
            group_average(gvar_ps, part_var, spread[:, 0:2], 0)
            pe.wait_ge(q_lo_done, 3)
            image(0, False)
            with pe.Fori(1, B - 1) as i:
                image(i, False)
            image(B - 1, True)


def attend(nc, qk_hi, qk_lo, v_pairs, rel_tables, one_hots, identity, rel_scratch, den_scratch, rec_scratch, o_pairs,
           proj_w_t, wp_hi, wp_lo):
    q_hi_d, k_hi_d = qk_hi
    q_lo_d, k_lo_d = qk_lo
    SLOTS = 4
    with ExitStack() as ctx:
        sb = lambda name, shape, dt: ctx.enter_context(nc.sbuf_tensor(name, shape, dt))
        pb = lambda name, shape: ctx.enter_context(nc.psum_tensor(name, shape, F32))
        sem = lambda name: ctx.enter_context(nc.semaphore(name))
        two = lambda name, shape, dt: [sb(f"{name}{i}", shape, dt) for i in range(2)]
        q_hi = two("q_hi", [P, 2, T], F32R)
        q_lo = two("q_lo", [P, 2, T], F32R)
        q_max = two("q_max", [P, 2, T], F32R)
        k_hi = two("k_hi", [P, 2, T], F32R)
        k_lo = two("k_lo", [P, 2, T], F32R)
        v = two("v", [P, KB, P], F32)
        qp = sb("qp", [P, 2, T], F32R)
        table_hi = sb("table_hi", [P, P], F32R)
        table_lo = sb("table_lo", [P, P], F32R)
        offs = sb("offs", [P, 2, T], F32)
        rel = sb("rel", [P, T], F32)
        prob = sb("prob", [P, 2, SLOTS, T], F32)
        prob_sum = sb("prob_sum", [P, 2, T], F32)
        raw = sb("raw", [P, T], F32)
        den = sb("den", [P, T], F32)
        den_cols = sb("den_cols", [P, 2 * T // P], F32)
        rec_cols = sb("rec_cols", [P, 2 * T // P], F32)
        rec = sb("rec", [P, T], F32)
        o = sb("o", [P, T], F32)
        ones = sb("ones", [P, D], F32)
        ident = sb("ident", [P, P], F32)
        half_max = sb("half_max", [P, 4 * KB], F32)
        mx = sb("mx", [P, P], F32)
        mx_t = sb("mx_t", [2 * KB, P], F32R)
        ps_s = pb("ps_s", [P, 2, T])
        ps_o = pb("ps_o", [P, T])
        aux = pb("aux", [P, T])
        own = [slice(0, D), slice(D, P)]
        h_rows = [slice(D, D + HS), slice(0, HS)]
        w_rows = [slice(D + HS, P), slice(HS, D)]
        max_row = [slice(D, D + 1), slice(0, 1)]

        ones_rows, last_rec = sem("ones_rows"), sem("last_rec")
        tables_in, table_hi_done, tables_done = sem("tables_in"), sem("table_hi_done"), sem("tables_done")
        consts_in, one_hots_out, memsets = sem("consts_in"), sem("one_hots_out"), sem("memsets")
        qp_in, hi_in, lo_v_in, offs_stored, rel_in, max_rows_in, o_stored = (
            sem(n) for n in ("qp_in", "hi_in", "lo_v_in", "offs_stored", "rel_in", "max_rows_in", "o_stored"))
        den_stored, den_in, rec_stored, rec_in = (sem(n) for n in ("den_stored", "den_in", "rec_stored", "rec_in"))
        offs_done, offs_out = sem("offs_done"), sem("offs_out")
        q_copied = sem("q_copied")
        rel_hi_done = [sem("rel_hi_done0"), sem("rel_hi_done1")]
        rel_lo_done = [sem("rel_lo_done0"), sem("rel_lo_done1")]
        tile_done, max_done, max_ready, max_t_ps, max_t_done = (
            sem(n) for n in ("tile_done", "max_done", "max_ready", "max_t_ps", "max_t_done"))
        wp_raw = sb("wp_raw", [P, C], F32)
        wp_in, wp_hi_done, wp_lo_done = sem("wp_in"), sem("wp_hi_done"), sem("wp_lo_done")
        wp_part = {n: k for k, n in enumerate((0, 1, 2, NIT - 3, NIT - 2, NIT - 1))}
        s_done, exp_done, pv_done = sem("s_done"), sem("exp_done"), sem("pv_done")
        sums = [sem("sum0"), sem("sum1")]
        den_done, den_out, rec_small, raw_out, o_done = (
            sem(n) for n in ("den_done", "den_out", "rec_small", "raw_out", "o_done"))
        block = ctx.enter_context(nc.Block())

        SCORES = 2 * KB
        TILES = 2 * 2 * KB
        TILE_AT = ((), (), (4, 5, 6, 7)) + 3 * ((0, 2, 3, 5, 6, 7),) + ((0, 2, 4, 6, 7), (0, 2, 4, 5, 6))
        PER_STEP = [len(at) for at in TILE_AT]
        FIRST_TILE = [sum(PER_STEP[:kb]) for kb in range(KB)]
        MEMSETS = 7

        def pairs(engine, pair):
            for n in range(3):
                pair(n, n % 2)
            with engine.Fori(1, NIT // 2 - 2) as j:
                pair(2 * j + 1, 1)
                pair(2 * j + 2, 0)
            for n in range(NIT - 3, NIT):
                pair(n, n % 2)

        def rel_rows(n, s, e, axis):
            if axis == 0:
                return rel[h_rows[e], :], q_hi[s][h_rows[e], e, :], q_lo[s][h_rows[e], e, :]
            high, low = (x[s][w_rows[e], e, :].rearrange("p (h w) -> p h w", w=WS) for x in (q_hi, q_lo))
            return rel[w_rows[e], :].rearrange("p (w h) -> p h w", h=HS), high, low

        def rel_low(engine, n, s, e, axis):
            raw_rows, high, low = rel_rows(n, s, e, axis)
            engine.wait_ge(rel_hi_done[e], 2 * n + axis + 1)
            engine.tensor_tensor(low, raw_rows, words(high), ALU.subtract).then_inc(rel_lo_done[e], 1)

        def before(n, end):
            return not isinstance(n, int) or n < end

        @block.sync
        def _(sp):
            def load_qp(n):
                for part, src in enumerate((q_hi_d, q_lo_d)):
                    sp.dma_start(words(qp[own[part], :, :]), src[n].rearrange("(e p) t -> p e t", e=2)).then_inc(qp_in, 16)

            sp.wait_ge(memsets, 1)
            for a, table in enumerate(rel_tables):
                for e in range(2):
                    sp.dma_start(offs[own[e], 0, a * D:a * D + NREL], table).then_inc(tables_in, 16)
            load_qp(0)
            for e in range(2):
                sp.dma_start(raw[own[e], :], one_hots).then_inc(consts_in, 16)
            sp.dma_start(ident[:, :], identity).then_inc(consts_in, 16)

            def load_high(n, s):
                for e in range(2):
                    for dst, src in ((q_hi, q_hi_d), (k_hi, k_hi_d)):
                        sp.dma_start(words(dst[s][own[e], e, :]), src[n][own[e], :]).then_inc(hi_in, 16)

            def load_low(n, s):
                for dst, src in ((q_lo, q_lo_d), (k_lo, k_lo_d)):
                    for e in range(2):
                        sp.dma_start(words(dst[s][own[e], e, :]), src[n][own[e], :]).then_inc(lo_v_in, 16)

            def load_v(n, s):
                sp.dma_start(v[s][:, :, :], v_pairs[n]).then_inc(lo_v_in, 16)

            def store_offs(n, s):
                for e in range(2):
                    sp.wait_ge(offs_out, 8 * n + 4 * (e + 1))
                    sp.dma_start(rel_scratch[s, e], offs[:, e, :]).then_inc(offs_stored, 16)

            def load_rel(n, s):
                sp.wait_ge(offs_stored, 32 * (n + 1))
                for a, rows in enumerate((h_rows, w_rows)):
                    for e in range(2):
                        src = bass.AP(rel_scratch.tensor, ((2 * s + e) * P + a * D) * T, [[T, HS], [T + WS, HS], [1, WS]])
                        sp.dma_start(rel[rows[e], :].rearrange("p (a b) -> p a b", b=WS), src).then_inc(rel_in, 16)

            def load_max_rows(n, s):
                sp.wait_ge(max_t_done, n + 1)
                for e in range(2):
                    dst = words(q_max[s][max_row[e], e, :]).rearrange("p (a b) -> p a b", b=P)
                    sp.dma_start(dst, words(mx_t[e * KB:(e + 1) * KB, :])).then_inc(max_rows_in, 16)

            def reshape_denominators(n):
                sp.wait_ge(den_out, n + 1)
                sp.dma_start(den_scratch, den[0:P:D, :]).then_inc(den_stored, 16)
                sp.wait_ge(den_stored, 16 * (n + 1))
                sp.dma_start(den_cols[:, :], den_scratch.rearrange("e (p j) -> (e p) j", j=2 * T // P)).then_inc(den_in, 16)
                sp.wait_ge(rec_small, n + 1)
                sp.dma_start(rec_scratch.rearrange("e (p j) -> (e p) j", j=2 * T // P), rec_cols[:, :]).then_inc(rec_stored, 16)
                if positive(n):
                    sp.wait_ge(o_done, n)
                sp.wait_ge(rec_stored, 16 * (n + 1))
                for e in range(2):
                    src = bass.AP(rec_scratch.tensor, e * T, [[0, D], [1, T]])
                    sp.dma_start(rec[own[e], :], src).then_inc(rec_in, 16)

            def store_o(n):
                sp.wait_ge(o_done, n + 1)
                sp.dma_start(o_pairs[n], o[:, :]).then_inc(o_stored, 16)

            sp.wait_ge(memsets, MEMSETS)
            load_high(0, 0)
            store_offs(0, 0)
            load_qp(1)
            load_rel(0, 0)
            load_low(0, 0)
            load_v(0, 0)
            store_offs(1, 1)
            load_qp(2)
            for e in range(2):
                sp.wait_ge(rel_lo_done[e], 2)
            load_rel(1, 1)
            load_max_rows(0, 0)

            def pair(n, s):
                if before(n, NIT - 1):
                    if positive(SCORES * n):
                        sp.wait_ge(s_done, SCORES * n)
                    load_high(n + 1, 1 - s)
                if before(n, NIT - 2):
                    store_offs(n + 2, s)
                if before(n, NIT - 1):
                    load_low(n + 1, 1 - s)
                    if positive(KB * n):
                        sp.wait_ge(pv_done, KB * n)
                    load_v(n + 1, 1 - s)
                if positive(n):
                    reshape_denominators(n - 1)
                if positive(n - 1):
                    store_o(n - 2)
                if before(n, NIT - 2):
                    for e in range(2):
                        sp.wait_ge(rel_lo_done[e], 2 * (n + 2))
                if isinstance(n, int):
                    k = wp_part[n]
                    if k > 0:
                        sp.wait_ge(wp_lo_done, k)
                    sp.dma_start(wp_raw[:, :], proj_w_t[k * P:(k + 1) * P, :]).then_inc(wp_in, 16)
                if before(n, NIT - 3):
                    load_qp(n + 3)
                if before(n, NIT - 2):
                    load_rel(n + 2, s)
                if before(n, NIT - 1):
                    load_max_rows(n + 1, 1 - s)
            pairs(sp, pair)
            store_o(NIT - 2)
            store_o(NIT - 1)
            sp.wait_ge(o_stored, 16 * NIT)

        @block.gpsimd
        def _(pool):
            def low_rows(n, s, axis):
                rel_low(pool, n, s, 1, axis)
                pool.wait_ge(rel_lo_done[1], 2 * n + axis + 1)

            nc.gpsimd.memset(offs[:, 0, 0:P], 0.0).then_inc(memsets, 1)
            nc.gpsimd.memset(ones[:, :], 1.0).then_inc(memsets, 1)
            for s in range(2):
                nc.gpsimd.memset(words(k_lo[s][:, :, :]), 0.0).then_inc(memsets, 1)
                nc.gpsimd.memset(words(q_max[s][:, :, :]), 0.0).then_inc(memsets, 1)
            nc.gpsimd.memset(mx[:, :], 0.0).then_inc(memsets, 1)
            pool.wait_ge(memsets, MEMSETS)
            low_rows(0, 0, 0)
            low_rows(0, 0, 1)

            def pair(n, s):
                for kb in range(1, KB):
                    if kb in (3, 4) and before(n, NIT - 1):
                        pool.wait_ge(sums[0], (KB - 1) * n + kb - 1)
                        low_rows(n + 1, 1 - s, kb - 3)
                    pool.wait_ge(exp_done, SCORES * n + 2 * kb + 1)
                    if kb == 1:
                        if positive(n):
                            pool.wait_ge(den_done, n)
                        nc.gpsimd.tensor_tensor(prob_sum[:, 0, :], prob[:, 0, 0, :], prob[:, 0, 1, :], ALU.add).then_inc(sums[0], 1)
                    else:
                        pool.wait_ge(sums[0], (KB - 1) * n + kb - 1)
                        nc.gpsimd.tensor_tensor(prob_sum[:, 0, :], prob_sum[:, 0, :], prob[:, 0, kb % SLOTS, :],
                                                ALU.add).then_inc(sums[0], 1)
            pairs(pool, pair)

        @block.scalar
        def _(act):
            act.wait_ge(tables_in, 16 * 4)
            nc.scalar.activation(table_hi[:, :], offs[:, 0, 0:P], ACT.Identity).then_inc(table_hi_done, 1)
            act.wait_ge(tables_done, 1)

            def copy_offs(n, chunks=range(4)):
                for c in chunks:
                    e, half = c // 2, c % 2
                    act.wait_ge(offs_done, 4 * n + c + 1)
                    if half == 0 and positive(n):
                        act.wait_ge(offs_stored, 32 * n)
                    cols = slice(half * HALF, (half + 1) * HALF)
                    nc.scalar.activation(offs[own[0], e, cols], aux[own[0], cols], ACT.Identity).then_inc(offs_out, 1)
                    nc.scalar.activation(offs[own[1], e, :].rearrange("p (w h) -> p h w", h=HS)[:, half * HS // 2:(half + 1) * HS // 2, :],
                                         aux[own[1], cols].rearrange("p (h w) -> p h w", w=WS), ACT.Identity).then_inc(offs_out, 1)

            def rel_high(n, s):
                act.wait_ge(rel_in, 64 * (n + 1))
                for axis in range(2):
                    raw_rows, high, _ = rel_rows(n, s, 1, axis)
                    nc.scalar.activation(high, raw_rows, ACT.Identity).then_inc(rel_hi_done[1], 1)

            def copy_q(n, s):
                act.wait_ge(hi_in, 16 * 4 * (n + 1))
                for e in range(2):
                    nc.scalar.activation(q_max[s][own[e], e, :], words(q_hi[s][own[e], e, :]), ACT.Identity).then_inc(q_copied, 1)

            def copy_output(n):
                act.wait_ge(pv_done, KB * (n + 1))
                if positive(n):
                    act.wait_ge(o_done, n)
                nc.scalar.activation(raw[:, :], ps_o[:, :], ACT.Identity).then_inc(raw_out, 1)

            def copy_denominators(n):
                act.wait_ge(den_done, n + 1)
                if positive(n):
                    act.wait_ge(den_stored, 16 * n)
                nc.scalar.activation(den[:, :], aux[:, :], ACT.Identity).then_inc(den_out, 1)

            copy_offs(0)
            act.wait_ge(consts_in, 16 * 3)
            for s in range(2):
                for e in range(2):
                    nc.scalar.activation(k_hi[s][own[1 - e], e, :], raw[own[1 - e], :], ACT.Identity).then_inc(one_hots_out, 1)
            copy_offs(1)
            rel_high(0, 0)
            copy_q(0, 0)

            def exp(n, kb, e):
                act.wait_ge(s_done, SCORES * n + 2 * kb + e + 1)
                if positive(KB * n + kb - SLOTS + 1):
                    act.wait_ge(pv_done, KB * n + kb - SLOTS + 1)
                    summed = max(kb - SLOTS, 1) if kb >= SLOTS else kb - SLOTS + 1
                    act.wait_ge(sums[e], (KB - 1) * n + summed)
                nc.scalar.activation(prob[:, e, kb % SLOTS, :], ps_s[:, e, :], ACT.Exp).then_inc(exp_done, 1)

            def pair(n, s):
                for kb in range(KB):
                    for e in range(2):
                        if kb == 0 and before(n, NIT - 2):
                            copy_offs(n + 2, (e,))
                        exp(n, kb, e)
                    if kb == 0 and positive(n):
                        copy_output(n - 1)
                    if kb == 0 and before(n, NIT - 2):
                        copy_offs(n + 2, (2, 3))
                    if kb == 1 and positive(n):
                        copy_denominators(n - 1)
                    if kb == 2 and before(n, NIT - 1):
                        rel_high(n + 1, 1 - s)
                    if kb == 3 and before(n, NIT - 1):
                        copy_q(n + 1, 1 - s)
                    if kb == 5 and isinstance(n, int):
                        k = wp_part[n]
                        act.wait_ge(wp_in, 16 * (k + 1))
                        nc.scalar.activation(wp_hi[:, k, :], wp_raw[:, :], ACT.Identity).then_inc(wp_hi_done, 1)
            pairs(act, pair)
            copy_output(NIT - 1)

        @block.vector
        def _(dve):
            dve.wait_ge(table_hi_done, 1)
            nc.vector.tensor_tensor(table_lo[:, :], offs[:, 0, 0:P], words(table_hi[:, :]), ALU.subtract).then_inc(tables_done, 1)
            dve.wait_ge(memsets, MEMSETS)
            for s in range(2):
                for e in range(2):
                    nc.vector.memset(words(k_lo[s][max_row[e], e, :]), 1.0).then_inc(ones_rows, 1)

            def split_rel(n, s):
                dve.wait_ge(rel_in, 64 * (n + 1))
                if positive(SCORES * (n - 1)):
                    dve.wait_ge(s_done, SCORES * (n - 1))
                for axis in range(2):
                    raw_rows, high, _ = rel_rows(n, s, 0, axis)
                    nc.vector.tensor_copy(high, raw_rows).then_inc(rel_hi_done[0], 1)
                for axis in range(2):
                    rel_low(dve, n, s, 0, axis)

            def row_max(n, t):
                dve.wait_ge(tile_done, TILES * n + t + 1)
                if t == 0 and positive(n):
                    dve.wait_ge(max_ready, n)
                nc.vector.reduce_max(half_max[:, t:t + 1], aux[:, (t % 2) * HALF:(t % 2 + 1) * HALF], AX_X).then_inc(max_done, 1)

            def negate_max(n):
                dve.wait_ge(max_done, TILES * (n + 1))
                if positive(n):
                    dve.wait_ge(max_t_ps, n)
                nc.vector.reduce_max(mx[:, 0:2 * KB], half_max[:, :].rearrange("p (t h) -> p t h", h=2), AX_X).then_inc(max_ready, 1)
                dve.wait_ge(max_t_ps, n + 1)
                if positive(n):
                    dve.wait_ge(max_rows_in, 32 * n)
                nc.vector.tensor_scalar(mx_t[:, :], aux[0:2 * KB, 0:P], -1.0, None, ALU.mult).then_inc(max_t_done, 1)

            def add(n, kb):
                dve.wait_ge(exp_done, SCORES * n + 2 * kb + 2)
                if kb == 1:
                    if positive(n):
                        dve.wait_ge(den_done, n)
                    nc.vector.tensor_tensor(prob_sum[:, 1, :], prob[:, 1, 0, :], prob[:, 1, 1, :], ALU.add).then_inc(sums[1], 1)
                else:
                    dve.wait_ge(sums[1], (KB - 1) * n + kb - 1)
                    nc.vector.tensor_tensor(prob_sum[:, 1, :], prob_sum[:, 1, :], prob[:, 1, kb % SLOTS, :],
                                            ALU.add).then_inc(sums[1], 1)

            def invert_denominators(n):
                dve.wait_ge(den_in, 16 * (n + 1))
                if positive(n):
                    dve.wait_ge(rec_stored, 16 * n)
                nc.vector.reciprocal(rec_cols[:, :], den_cols[:, :]).then_inc(rec_small, 1)

            def normalise(n):
                dve.wait_ge(rec_in, 32 * (n + 1))
                dve.wait_ge(raw_out, n + 1)
                if positive(n):
                    dve.wait_ge(o_stored, 16 * n)
                nc.vector.tensor_tensor(o[:, :], raw[:, :], rec[:, :], ALU.mult).then_inc(o_done, 1)

            split_rel(0, 0)
            for u in range(2 * KB):
                dve.wait_ge(tile_done, 2 * (u + 1))
                nc.vector.reduce_max(half_max[:, 2 * u:2 * u + 2], ps_s[:, u % 2, :].rearrange("p (h t) -> p h t", h=2),
                                     AX_X).then_inc(max_done, 2)
            negate_max(0)

            def pair(n, s):
                if positive(n):
                    add(n - 1, KB - 2)
                    add(n - 1, KB - 1)
                if positive(n - 1):
                    normalise(n - 2)
                if before(n, NIT - 1):
                    split_rel(n + 1, 1 - s)
                for kb in range(1, KB):
                    tiles = range(FIRST_TILE[kb], FIRST_TILE[kb] + PER_STEP[kb]) if before(n, NIT - 1) else ()
                    for t in tiles[:-1]:
                        row_max(n + 1, t)
                    if 2 <= kb < KB - 1:
                        add(n, kb - 1)
                    for t in tiles[-1:]:
                        row_max(n + 1, t)
                    if kb == 4 and positive(n):
                        invert_denominators(n - 1)
                    if kb == 6 and isinstance(n, int):
                        k = wp_part[n]
                        dve.wait_ge(wp_hi_done, k + 1)
                        nc.vector.tensor_tensor(wp_lo[:, k, :], wp_raw[:, :], words(wp_hi[:, k, :]),
                                                ALU.subtract).then_inc(wp_lo_done, 1)
                if before(n, NIT - 1):
                    negate_max(n + 1)
            pairs(dve, pair)
            add(NIT - 1, KB - 2)
            add(NIT - 1, KB - 1)
            normalise(NIT - 2)
            dve.wait_ge(den_done, NIT)
            dve.wait_ge(o_done, NIT - 1)
            nc.vector.reciprocal(rec[:, :], aux[:, :]).then_inc(last_rec, 1)
            dve.wait_ge(last_rec, 1)
            dve.wait_ge(raw_out, NIT)
            dve.wait_ge(o_stored, 16 * (NIT - 1))
            nc.vector.tensor_tensor(o[:, :], raw[:, :], rec[:, :], ALU.mult).then_inc(o_done, 1)

        @block.tensor
        def _(pe):
            def offsets(n, chunks=range(4)):
                pe.wait_ge(qp_in, 32 * (n + 1))
                for c in chunks:
                    e, half = c // 2, c % 2
                    cols = slice(half * HALF, (half + 1) * HALF)
                    if c < 2:
                        if positive(n - 1):
                            pe.wait_ge(max_t_done, n - 1)
                        elif isinstance(n, int) and n == 1:
                            pe.wait_ge(offs_out, 8)
                    else:
                        pe.wait_ge(offs_out, 8 * n + 2 * (c - 1))
                    nc.tensor.matmul(aux[:, cols], table_hi[:, :], qp[:, e, cols], start=True, stop=False)
                    nc.tensor.matmul(aux[:, cols], table_lo[:, :], qp[:, e, cols], start=False, stop=True).then_inc(offs_done, 1)

            def max_tile(n, s, t):
                e, qb, half = t // (2 * KB), t // 2 % KB, t % 2
                if t == 0:
                    if before(n, NIT - 1):
                        pe.wait_ge(offs_out, 8 * (n + 2))
                    if positive(n - 1):
                        pe.wait_ge(den_out, n - 1)
                    pe.wait_ge(hi_in, 16 * 4 * (n + 1))
                if t >= 2:
                    pe.wait_ge(max_done, TILES * n + t - 1)
                if t % (2 * KB) == 0:
                    pe.wait_ge(rel_hi_done[e], 2 * (n + 1))
                mm = nc.tensor.matmul(aux[:, half * HALF:(half + 1) * HALF], q_hi[s][:, e, qb * P:(qb + 1) * P],
                                      k_hi[s][:, e, half * HALF:(half + 1) * HALF], start=True, stop=True)
                mm.then_inc(tile_done, 1)

            def transpose_max(n):
                pe.wait_ge(max_ready, n + 1)
                nc.tensor.transpose(aux[:, 0:P], mx[:, :], ident[:, :]).then_inc(max_t_ps, 1)

            def scores(n, s, e, kb, j):
                keys = slice(kb * P, (kb + 1) * P)
                if j == 0:
                    if kb == 0 and e == 0:
                        pe.wait_ge(lo_v_in, 16 * 5 * (n + 1))
                        for i in range(2):
                            pe.wait_ge(rel_lo_done[i], 2 * (n + 1))
                        pe.wait_ge(q_copied, 2 * (n + 1))
                    if positive(SCORES * n + 2 * (kb - 1) + e + 1):
                        pe.wait_ge(exp_done, SCORES * n + 2 * (kb - 1) + e + 1)
                if j == 2 and kb == 0 and e == 0:
                    pe.wait_ge(max_rows_in, 32 * (n + 1))
                k, q = ((k_hi, q_hi), (k_hi, q_lo), (k_lo, q_max))[j]
                for half in range(2):
                    cols = slice(half * HALF, (half + 1) * HALF)
                    mm = nc.tensor.matmul(ps_s[:, e, cols], k[s][:, e, keys], q[s][:, e, cols],
                                          start=(j == 0), stop=(j == 2))
                if j == 2:
                    mm.then_inc(s_done, 1)

            def values(n, s, kb):
                pe.wait_ge(exp_done, SCORES * n + 2 * kb + 2)
                for half in range(2):
                    for e in range(2):
                        cols = slice(half * HALF, (half + 1) * HALF)
                        mm = nc.tensor.matmul(ps_o[own[e], cols], v[s][:, kb, own[e]], prob[:, e, kb % SLOTS, cols],
                                              start=(kb == 0), stop=(kb == KB - 1))
                mm.then_inc(pv_done, 1)

            def denominators(n):
                if before(n, NIT - 3):
                    pe.wait_ge(offs_out, 8 * (n + 4))
                if before(n, NIT - 1):
                    pe.wait_ge(max_t_done, n + 2)
                for e in range(2):
                    pe.wait_ge(sums[e], (KB - 1) * (n + 1))
                for half in range(2):
                    for e in range(2):
                        cols = slice(half * HALF, (half + 1) * HALF)
                        mm = nc.tensor.matmul(aux[own[e], cols], ones[:, :], prob_sum[:, e, cols], start=True, stop=True)
                mm.then_inc(den_done, 1)

            pe.wait_ge(tables_done, 1)
            offsets(0)
            offsets(1)
            pe.wait_ge(memsets, MEMSETS)
            pe.wait_ge(one_hots_out, 4)
            pe.wait_ge(ones_rows, 4)
            pe.wait_ge(hi_in, 16 * 4)
            for u in range(2 * KB):
                e, qb = u // KB, u % KB
                if qb == 0:
                    pe.wait_ge(rel_hi_done[e], 2)
                if u >= 2:
                    pe.wait_ge(max_done, 2 * (u - 1))
                for half in range(2):
                    cols = slice(half * HALF, (half + 1) * HALF)
                    mm = nc.tensor.matmul(ps_s[:, u % 2, cols], q_hi[0][:, e, qb * P:(qb + 1) * P], k_hi[0][:, e, cols],
                                          start=True, stop=True)
                mm.then_inc(tile_done, 2)
            transpose_max(0)

            def first_step(n, s):
                more = before(n, NIT - 2)
                for e in range(2):
                    scores(n, s, e, 0, 0)
                    scores(n, s, e, 0, 1)
                if more:
                    offsets(n + 2, (0,))
                if positive(n):
                    values(n - 1, 1 - s, KB - 1)
                scores(n, s, 0, 0, 2)
                if more:
                    offsets(n + 2, (1, 2))
                scores(n, s, 1, 0, 2)

            def step(n, s, kb):
                t = FIRST_TILE[kb]

                def tile(place):
                    nonlocal t
                    if place in TILE_AT[kb] and before(n, NIT - 1):
                        max_tile(n + 1, 1 - s, t)
                        t += 1
                for i in range(6):
                    tile(i)
                    if kb == 1 and i == 3 and before(n, NIT - 2):
                        offsets(n + 2, (3,))
                    scores(n, s, i // 3, kb, i % 3)
                tile(6)
                if kb == 1 and positive(n):
                    pe.wait_ge(raw_out, n)
                values(n, s, kb - 1)
                if kb == 1 and positive(n):
                    denominators(n - 1)
                tile(7)
                if kb == KB - 1 and before(n, NIT - 1):
                    transpose_max(n + 1)

            def pair(n, s):
                first_step(n, s)
                for kb in range(1, KB):
                    step(n, s, kb)
            pairs(pe, pair)
            values(NIT - 1, 1, KB - 1)
            denominators(NIT - 1)


def project_out(nc, x_t, o_pairs, w_hi, w_lo, v_bias_cols, bias_cols, out_t):
    with ExitStack() as ctx:
        sb = lambda name, shape, dt: ctx.enter_context(nc.sbuf_tensor(name, shape, dt))
        sem = lambda name: ctx.enter_context(nc.semaphore(name))
        o_raw = sb("o_raw", [P, 2, CB, HALF], F32)
        o_hi = sb("o_hi", [P, 2, CB, HALF], F32R)
        o_lo = sb("o_lo", [P, 2, CB, HALF], F32R)
        x_res = sb("x_res", [P, 2, CB, HALF], F32)
        y = sb("y", [P, CB, HALF], F32)
        v_bias = sb("o_bias", [P, CB], F32)
        bias = sb("p_bias", [P, CB], F32)
        ps = ctx.enter_context(nc.psum_tensor("ps_y", [P, CB, HALF], F32))
        bias_in = sem("p3_bias_in")
        o_in = [sem(f"o_in{i}") for i in range(2)]
        x_in = [sem(f"res_in{i}") for i in range(2)]
        o_hi_done, o_lo_done = sem("o_hi_done"), sem("o_lo_done")
        block_done, y_done = sem("block_done"), sem("y_done")
        y_stored = [sem(f"y_stored{i}") for i in range(CB)]
        block = ctx.enter_context(nc.Block())

        @block.sync
        def _(sp):
            def load_o(i, h):
                cols = slice(h * HALF, (h + 1) * HALF)
                sp.dma_start(o_raw[:, h], o_pairs[i].rearrange("j p t -> p j t")[:, :, cols]).then_inc(o_in[h], 16)

            def load_x(i, h):
                cols = slice(h * HALF, (h + 1) * HALF)
                sp.dma_start(x_res[:, h], x_t[i].rearrange("(k p) t -> p k t", p=P)[:, :, cols]).then_inc(x_in[h], 16)

            load_o(0, 0)
            sp.dma_start(v_bias[:, :], v_bias_cols).then_inc(bias_in, 16)
            sp.dma_start(bias[:, :], bias_cols).then_inc(bias_in, 16)
            load_o(0, 1)
            load_x(0, 0)
            load_x(0, 1)

            def image(i, last):
                for h in range(2):
                    n = 2 * i + h
                    for g in range(CB):
                        sp.wait_ge(y_done, n * CB + g + 1)
                        sp.dma_start(out_t[i, g * P:(g + 1) * P, h * HALF:(h + 1) * HALF], y[:, g, :]).then_inc(y_stored[g], 16)
                    if not last:
                        sp.wait_ge(o_lo_done, n + 1)
                        load_o(i + 1, h)
                        load_x(i + 1, h)
            image(0, False)
            with sp.Fori(1, B - 1) as i:
                image(i, False)
            image(B - 1, True)
            for g in range(CB):
                sp.wait_ge(y_stored[g], 16 * 2 * B)

        @block.scalar
        def _(act):
            act.wait_ge(bias_in, 32)

            def split_hi(i, h, n):
                act.wait_ge(o_in[h], 16 * (i + 1))
                if not (isinstance(n, int) and n < 2):
                    act.wait_ge(block_done, (n - 1) * CB)
                for k in range(CB):
                    nc.scalar.activation(o_hi[:, h, k, :], o_raw[:, h, k, :], ACT.Identity,
                                         bias=v_bias[:, k:k + 1]).then_inc(o_hi_done, 1)
            split_hi(0, 0, 0)
            split_hi(0, 1, 1)
            with act.Fori(0, B - 1) as i:
                for h in range(2):
                    split_hi(i + 1, h, 2 * i + 2 + h)

        @block.vector
        def _(dve):
            dve.wait_ge(bias_in, 32)

            def split_lo(n, h):
                for k in range(CB):
                    dve.wait_ge(o_hi_done, n * CB + k + 1)
                    op = nc.vector.scalar_tensor_tensor(o_lo[:, h, k, :], o_raw[:, h, k, :], v_bias[:, k:k + 1],
                                                        words(o_hi[:, h, k, :]), ALU.add, ALU.subtract)
                op.then_inc(o_lo_done, 1)

            def finish(i, n, h):
                for g in range(CB):
                    dve.wait_ge(block_done, n * CB + g + 1)
                    if g == 0:
                        dve.wait_ge(x_in[h], 16 * (i + 1))
                    if positive(16 * n):
                        dve.wait_ge(y_stored[g], 16 * n)
                    nc.vector.scalar_tensor_tensor(y[:, g, :], ps[:, g, :], bias[:, g:g + 1], x_res[:, h, g, :],
                                                   ALU.add, ALU.add).then_inc(y_done, 1)
            split_lo(0, 0)
            split_lo(1, 1)

            def image(i):
                for h in range(2):
                    finish(i, 2 * i + h, h)
                    split_lo(2 * i + h + 2, h)
            image(0)
            with dve.Fori(1, B - 1) as i:
                image(i)
            for h in range(2):
                finish(B - 1, 2 * (B - 1) + h, h)

        @block.tensor
        def _(pe):
            def image(i, first):
                for h in range(2):
                    n = 2 * i + h
                    pe.wait_ge(o_lo_done, n + 1)
                    for g in range(CB):
                        if not (first and h == 0):
                            pe.wait_ge(y_done, (n - 1) * CB + g + 1)
                        cols = slice(g * P, (g + 1) * P)
                        for k in range(CB):
                            for j, (w, o) in enumerate(((w_hi, o_hi), (w_hi, o_lo), (w_lo, o_hi))):
                                mm = nc.tensor.matmul(ps[:, g, :], w[:, k, cols], o[:, h, k, :],
                                                      start=(k == 0 and j == 0), stop=(k == CB - 1 and j == 2))
                        mm.then_inc(block_done, 1)
            image(0, True)
            with pe.Fori(1, B) as i:
                image(i, False)


def build(nc, io):
    scratch = lambda name, shape: nc.dram_tensor(name, shape, F32, kind="Internal").ap()
    qk_hi = [scratch(f"{n}_hi_d", (NIT, P, T)) for n in "qk"]
    qk_lo = [scratch(f"{n}_lo_d", (NIT, P, T)) for n in "qk"]
    v_d = scratch("v_d", (NIT, P, KB, P))
    rel_scratch = scratch("rel_d", (2, 2, P, T))
    den_scratch, rec_scratch = scratch("den_d", (2, T)), scratch("rec_d", (2, T))
    o_d = scratch("o_d", (NIT, P, T))
    by_image = lambda ap: ap.rearrange("(i j) p t -> i (j p) t", j=NPAIR)
    project_qkv(nc, io["x_t"], io["qkv_w_t"], io["qk_bias"], io["group_mean"],
                [by_image(a) for a in qk_hi], [by_image(a) for a in qk_lo],
                v_d.rearrange("(i j) p k d -> i j p k d", j=NPAIR))
    with ExitStack() as ctx:
        wp_hi, wp_lo = (ctx.enter_context(nc.sbuf_tensor(name, [P, CB, C], F32R)) for name in ("wp_hi", "wp_lo"))
        attend(nc, qk_hi, qk_lo, v_d, (io["rel_h_t"], io["rel_w_t"]), io["one_hots"], io["identity"], rel_scratch,
               den_scratch, rec_scratch, o_d, io["proj_w_t"], wp_hi, wp_lo)
        project_out(nc, io["x_t"], o_d.rearrange("(i j) p t -> i j p t", j=NPAIR), wp_hi, wp_lo, io["v_bias"],
                    io["proj_bias"], io["out_t"])


def shape_constants():
    q = np.arange(P) // PER_GROUP
    token = np.arange(T)
    j = np.arange(HS)[:, None]
    return {
        "group_mean": (q[:, None] == q[None, :]).astype(np.float32) / PER_GROUP,
        "one_hots": np.concatenate([HS - 1 - j == token // WS, WS - 1 - j == token % WS]).astype(np.float32),
        "identity": np.eye(P, dtype=np.float32),
    }


def kernel(x, L0_conv_qkv_w, L0_conv_qkv_b, L0_conv_proj_w, L0_conv_proj_b, L0_conv_rel_pos_h, L0_conv_rel_pos_w):
    import concourse.bacc as bacc
    from concourse.bass_utils import run_bass_kernel_spmd

    cols = lambda v: np.ascontiguousarray(np.asarray(v).reshape(-1, P).T)
    qkv_b = np.asarray(L0_conv_qkv_b)
    arrays = {
        "x_t": np.ascontiguousarray(np.asarray(x).reshape(B, T, C).transpose(0, 2, 1)),
        "qkv_w_t": np.ascontiguousarray(np.asarray(L0_conv_qkv_w).T),
        "proj_w_t": np.ascontiguousarray(np.asarray(L0_conv_proj_w).T),
        "qk_bias": cols(qkv_b[:2 * C]),
        "v_bias": cols(qkv_b[2 * C:]),
        "proj_bias": cols(L0_conv_proj_b),
        "rel_h_t": np.ascontiguousarray(np.asarray(L0_conv_rel_pos_h).T),
        "rel_w_t": np.ascontiguousarray(np.asarray(L0_conv_rel_pos_w).T),
        **shape_constants(),
    }
    nc = bacc.Bacc("TRN2", target_bir_lowering=False, num_devices=1)
    io = {n: nc.dram_tensor(n, a.shape, F32, kind="ExternalInput").ap() for n, a in arrays.items()}
    io["out_t"] = nc.dram_tensor("out_t", (B, C, T), F32, kind="ExternalOutput").ap()
    build(nc, io)
    result = run_bass_kernel_spmd(nc, [arrays], core_ids=[0])
    out = result.results[0]["out_t"]
    return np.ascontiguousarray(out.transpose(0, 2, 1)).reshape(B, HS, WS, C)
```
